# Optimizing a Trainium2 kernel written in Bass

```python
import numpy as np
import jax
import jax.numpy as jnp

def _softmax(x, axis=-1):
    return jax.nn.softmax(x, axis=axis)

def _gelu(x):
    return jax.nn.gelu(x, approximate=True)

def _silu(x):
    return jax.nn.silu(x)

def _sigmoid(x):
    return jax.nn.sigmoid(x)

def _layernorm(x, axis=-1, eps=1e-05):
    m = jnp.mean(x, axis=axis, keepdims=True)
    v = jnp.var(x, axis=axis, keepdims=True)
    return (x - m) / jnp.sqrt(v + eps)

def _scatter_add(tgt, idx, src, axis=0):
    return tgt.at[idx].add(src)

def _segment_sum(src, seg, n):
    return jax.ops.segment_sum(src, seg, n)
kernel_name = 'mk_metaformer_d1_conv_nchw384_r4_c982e1'

def setup_inputs(seed: int=0):
    np.random.seed(seed)
    _w = jnp.asarray

    def _rec_inputs():
        import jax
        import jax.numpy as jnp
        _gk = jax.random.key(seed)
        x = -9.309e-05 + 1 * jax.random.normal(jax.random.fold_in(_gk, 1), (4, 96, 56, 56), jnp.float32)
        return x
    x = _rec_inputs()

    def _L0_conv_setup():
        import jax, jax.numpy as jnp
        import numpy as np
        from jax import lax
        B, C, H, W = (4, 96, 56, 56)
        NH, HC, STRIDE = (12, 32, 2)
        SCALE = HC ** (-0.5)

        def _dwconv(x, w, b, stride):
            y = lax.conv_general_dilated(x, w, (stride, stride), [(1, 1), (1, 1)], dimension_numbers=('NCHW', 'OIHW', 'NCHW'), feature_group_count=x.shape[1])
            return y + b[None, :, None, None]

        def _grid_sample_bilinear(value, grid):
            Hh, Ww = (value.shape[2], value.shape[3])
            ix = (grid[..., 0] + 1.0) * 0.5 * (Ww - 1)
            iy = (grid[..., 1] + 1.0) * 0.5 * (Hh - 1)
            x0 = jnp.floor(ix)
            y0 = jnp.floor(iy)
            wx = ix - x0
            wy = iy - y0
            x0i = jnp.clip(x0, 0, Ww - 1).astype(jnp.int32)
            x1i = jnp.clip(x0 + 1, 0, Ww - 1).astype(jnp.int32)
            y0i = jnp.clip(y0, 0, Hh - 1).astype(jnp.int32)
            y1i = jnp.clip(y0 + 1, 0, Hh - 1).astype(jnp.int32)

            def per_b(img, y0i, y1i, x0i, x1i, wx, wy):
                v00 = img[:, y0i, x0i]
                v01 = img[:, y0i, x1i]
                v10 = img[:, y1i, x0i]
                v11 = img[:, y1i, x1i]
                return v00 * (1 - wx) * (1 - wy) + v01 * wx * (1 - wy) + v10 * (1 - wx) * wy + v11 * wx * wy
            return jax.vmap(per_b)(value, y0i, y1i, x0i, x1i, wx, wy)

        def _ref_points(Hk, Wk):
            ref_y = jnp.linspace(0.5, Hk - 0.5, Hk)
            ref_x = jnp.linspace(0.5, Wk - 0.5, Wk)
            ry, rx = jnp.meshgrid(ref_y, ref_x, indexing='ij')
            return jnp.stack([ry / Hk * 2 - 1, rx / Wk * 2 - 1], axis=-1)
        key = jax.random.key(seed)
        ks = jax.random.split(key, 10)
        s = 0.05
        return {'x': jax.random.normal(ks[0], (B, C, H, W), jnp.float32), 'w_v': jax.random.normal(ks[1], (C, 1, 3, 3), jnp.float32) * s, 'b_v': jnp.zeros((C,), jnp.float32), 'w_q': jax.random.normal(ks[2], (C, 1, 3, 3), jnp.float32) * s, 'b_q': jnp.zeros((C,), jnp.float32), 'w_k': jax.random.normal(ks[3], (C, 1, 3, 3), jnp.float32) * s, 'b_k': jnp.zeros((C,), jnp.float32), 'w_off1': jax.random.normal(ks[4], (C, 1, 3, 3), jnp.float32) * s, 'b_off1': jnp.zeros((C,), jnp.float32), 'ln_g': jnp.ones((C,), jnp.float32), 'ln_b': jnp.zeros((C,), jnp.float32), 'w_off2': jax.random.normal(ks[5], (2, C), jnp.float32) * s, 'w_out': jax.random.normal(ks[6], (C, C), jnp.float32) * s}
    _L0_conv_all = _L0_conv_setup()
    _L0_conv_in = {k: v for k, v in _L0_conv_all.items() if k in ('w_v', 'b_v', 'w_q', 'b_q', 'w_k', 'b_k', 'w_off1', 'b_off1', 'ln_g', 'ln_b', 'w_off2', 'w_out')}
    del _L0_conv_all

    def _L0_ffn_setup():
        import jax, jax.numpy as jnp
        import numpy as np
        NUM_EXPERTS = 4
        TOP_K = 2
        DIM = 96
        HID = 4 * DIM
        key = jax.random.key(seed)
        ks = jax.random.split(key, 5)
        B, S = (16, 512)
        scale_in = 1.0 / np.sqrt(DIM)
        scale_hid = 1.0 / np.sqrt(HID)
        return {'x': jax.random.normal(ks[0], (B, S, DIM), dtype=jnp.float32), 'gate_w': jax.random.normal(ks[1], (DIM, NUM_EXPERTS), dtype=jnp.float32) * scale_in, 'gate_b': jnp.zeros((NUM_EXPERTS,), dtype=jnp.float32), 'w1': jax.random.normal(ks[2], (NUM_EXPERTS, DIM, HID), dtype=jnp.float32) * scale_in, 'b1': jnp.zeros((NUM_EXPERTS, HID), dtype=jnp.float32), 'w2': jax.random.normal(ks[3], (NUM_EXPERTS, HID, DIM), dtype=jnp.float32) * scale_hid, 'b2': jnp.zeros((NUM_EXPERTS, DIM), dtype=jnp.float32)}
    _L0_ffn_all = _L0_ffn_setup()
    _L0_ffn_in = {k: v for k, v in _L0_ffn_all.items() if k in ('gate_w', 'gate_b', 'w1', 'b1', 'w2', 'b2')}
    del _L0_ffn_all
    return {'x': x, 'L0_conv_w_v': _L0_conv_in['w_v'], 'L0_conv_b_v': _L0_conv_in['b_v'], 'L0_conv_w_q': _L0_conv_in['w_q'], 'L0_conv_b_q': _L0_conv_in['b_q'], 'L0_conv_w_k': _L0_conv_in['w_k'], 'L0_conv_b_k': _L0_conv_in['b_k'], 'L0_conv_w_off1': _L0_conv_in['w_off1'], 'L0_conv_b_off1': _L0_conv_in['b_off1'], 'L0_conv_ln_g': _L0_conv_in['ln_g'], 'L0_conv_ln_b': _L0_conv_in['ln_b'], 'L0_conv_w_off2': _L0_conv_in['w_off2'], 'L0_conv_w_out': _L0_conv_in['w_out'], 'L0_ffn_gate_w': _L0_ffn_in['gate_w'], 'L0_ffn_gate_b': _L0_ffn_in['gate_b'], 'L0_ffn_w1': _L0_ffn_in['w1'], 'L0_ffn_b1': _L0_ffn_in['b1'], 'L0_ffn_w2': _L0_ffn_in['w2'], 'L0_ffn_b2': _L0_ffn_in['b2']}

def reference(x, L0_conv_w_v, L0_conv_b_v, L0_conv_w_q, L0_conv_b_q, L0_conv_w_k, L0_conv_b_k, L0_conv_w_off1, L0_conv_b_off1, L0_conv_ln_g, L0_conv_ln_b, L0_conv_w_off2, L0_conv_w_out, L0_ffn_gate_w, L0_ffn_gate_b, L0_ffn_w1, L0_ffn_b1, L0_ffn_w2, L0_ffn_b2):
    import jax
    import jax.numpy as jnp

    def _L0_conv_ref(x, w_v, b_v, w_q, b_q, w_k, b_k, w_off1, b_off1, ln_g, ln_b, w_off2, w_out):
        import jax, jax.numpy as jnp
        import numpy as np
        from jax import lax
        B, C, H, W = (4, 96, 56, 56)
        NH, HC, STRIDE = (12, 32, 2)
        SCALE = HC ** (-0.5)

        def _dwconv(x, w, b, stride):
            y = lax.conv_general_dilated(x, w, (stride, stride), [(1, 1), (1, 1)], dimension_numbers=('NCHW', 'OIHW', 'NCHW'), feature_group_count=x.shape[1])
            return y + b[None, :, None, None]

        def _grid_sample_bilinear(value, grid):
            Hh, Ww = (value.shape[2], value.shape[3])
            ix = (grid[..., 0] + 1.0) * 0.5 * (Ww - 1)
            iy = (grid[..., 1] + 1.0) * 0.5 * (Hh - 1)
            x0 = jnp.floor(ix)
            y0 = jnp.floor(iy)
            wx = ix - x0
            wy = iy - y0
            x0i = jnp.clip(x0, 0, Ww - 1).astype(jnp.int32)
            x1i = jnp.clip(x0 + 1, 0, Ww - 1).astype(jnp.int32)
            y0i = jnp.clip(y0, 0, Hh - 1).astype(jnp.int32)
            y1i = jnp.clip(y0 + 1, 0, Hh - 1).astype(jnp.int32)

            def per_b(img, y0i, y1i, x0i, x1i, wx, wy):
                v00 = img[:, y0i, x0i]
                v01 = img[:, y0i, x1i]
                v10 = img[:, y1i, x0i]
                v11 = img[:, y1i, x1i]
                return v00 * (1 - wx) * (1 - wy) + v01 * wx * (1 - wy) + v10 * (1 - wx) * wy + v11 * wx * wy
            return jax.vmap(per_b)(value, y0i, y1i, x0i, x1i, wx, wy)

        def _ref_points(Hk, Wk):
            ref_y = jnp.linspace(0.5, Hk - 0.5, Hk)
            ref_x = jnp.linspace(0.5, Wk - 0.5, Wk)
            ry, rx = jnp.meshgrid(ref_y, ref_x, indexing='ij')
            return jnp.stack([ry / Hk * 2 - 1, rx / Wk * 2 - 1], axis=-1)
        Bx, Cx, Hx, Wx = x.shape
        value = _dwconv(x, w_v, b_v, 1)
        query = _dwconv(x, w_q, b_q, 1).reshape(Bx * NH, HC, -1)
        key = _dwconv(x, w_k, b_k, STRIDE).reshape(Bx * NH, HC, -1)
        off = _dwconv(x, w_off1, b_off1, STRIDE)
        o = jnp.transpose(off, (0, 2, 3, 1))
        mu = o.mean(-1, keepdims=True)
        var = o.var(-1, keepdims=True)
        o = (o - mu) / jnp.sqrt(var + 1e-05) * ln_g + ln_b
        o = jax.nn.gelu(o, approximate=False)
        offset = jnp.einsum('bhwc,pc->bhwp', o, w_off2)
        Hk, Wk = (offset.shape[1], offset.shape[2])
        ref = _ref_points(Hk, Wk)[None]
        pos = jnp.tanh(offset + ref)
        grid = pos[..., ::-1]
        v_sampled = _grid_sample_bilinear(value, grid)
        v_sampled = v_sampled.reshape(Bx * NH, HC, -1)
        attn = jnp.einsum('bcm,bcn->bmn', query, key) * SCALE
        out = jnp.einsum('bmn,bcn->bcm', attn, v_sampled)
        out = out.reshape(Bx, Cx, Hx, Wx)
        y = jnp.einsum('bchw,oc->bohw', out, w_out)
        return y

    def _L0_ffn_ref(x, gate_w, gate_b, w1, b1, w2, b2):
        import jax, jax.numpy as jnp
        import numpy as np
        NUM_EXPERTS = 4
        TOP_K = 2
        DIM = 96
        HID = 4 * DIM
        scores = jnp.einsum('bsd,de->bse', x, gate_w) + gate_b
        probs = jax.nn.softmax(scores, axis=-1)
        topk_vals, topk_idx = jax.lax.top_k(probs, TOP_K)
        mask = jnp.sum(jax.nn.one_hot(topk_idx, NUM_EXPERTS, dtype=probs.dtype), axis=-2)
        masked = probs * mask
        masked = masked / (jnp.sum(masked, axis=-1, keepdims=True) + 1e-09)
        h = jax.nn.gelu(jnp.einsum('bsd,edh->ebsh', x, w1) + b1[:, None, None, :], approximate=False)
        y = jnp.einsum('ebsh,ehd->ebsd', h, w2) + b2[:, None, None, :]
        out = jnp.einsum('bse,ebsd->bsd', masked, y)
        return out

    def _gn(v, G=32, eps=1e-05):
        B_, C_, H_, W_ = v.shape
        g = v.reshape(B_, G, C_ // G, H_, W_)
        m = jnp.mean(g, axis=(2, 3, 4), keepdims=True)
        s = jnp.var(g, axis=(2, 3, 4), keepdims=True)
        return ((g - m) / jnp.sqrt(s + eps)).reshape(v.shape)

    def _ln_c(v, eps=1e-06):
        m = jnp.mean(v, axis=1, keepdims=True)
        s = jnp.var(v, axis=1, keepdims=True)
        return (v - m) / jnp.sqrt(s + eps)

    def _ln_t(v, eps=1e-05):
        m = jnp.mean(v, axis=-1, keepdims=True)
        s = jnp.var(v, axis=-1, keepdims=True)
        return (v - m) / jnp.sqrt(s + eps)

    def _to_tokens(v):
        B_, C_, H_, W_ = v.shape
        return v.reshape(B_, C_, H_ * W_).transpose(0, 2, 1)

    def _from_tokens(t, like):
        B_, C_, H_, W_ = like.shape
        return t.transpose(0, 2, 1).reshape(B_, C_, H_, W_)
    x = x + _L0_conv_ref(_ln_c(x), L0_conv_w_v, L0_conv_b_v, L0_conv_w_q, L0_conv_b_q, L0_conv_w_k, L0_conv_b_k, L0_conv_w_off1, L0_conv_b_off1, L0_conv_ln_g, L0_conv_ln_b, L0_conv_w_off2, L0_conv_w_out)
    t = _to_tokens(x)
    t = t + _L0_ffn_ref(_ln_t(t), L0_ffn_gate_w, L0_ffn_gate_b, L0_ffn_w1, L0_ffn_b1, L0_ffn_w2, L0_ffn_b2)
    x = _from_tokens(t, x)
    return x

_drawn_inputs = setup_inputs


def setup_inputs(seed=0):
    import zlib

    import numpy as np

    out = dict(_drawn_inputs(seed))
    spreads = {'L0_conv_b_v': (0.0, 0.1),
     'L0_conv_b_q': (0.0, 0.1),
     'L0_conv_b_k': (0.0, 0.1),
     'L0_conv_b_off1': (0.0, 0.1),
     'L0_conv_ln_g': (1.0, 0.2),
     'L0_conv_ln_b': (0.0, 0.1),
     'L0_ffn_gate_b': (0.0, 0.1),
     'L0_ffn_b1': (0.0, 0.1),
     'L0_ffn_b2': (0.0, 0.1)}
    factors = {}
    for name, (base, spread) in spreads.items():
        noise = np.random.default_rng([zlib.crc32(name.encode()), seed]).standard_normal(out[name].shape)
        drawn = base * np.exp(spread * noise) if base else spread * noise
        out[name] = jnp.asarray(drawn.astype(out[name].dtype))
    for name, factor in factors.items():
        out[name] = (out[name] * factor).astype(out[name].dtype)
    return out
```

```python
import concourse.bass as bass
from concourse import mybir
from contextlib import ExitStack

BATCH, C, H, W = 4, 96, 56, 56
PIX = H * W
HK, WK = H // 2, W // 2
SAMPLES = HK * WK
HEADS, HC = 12, 32
CH_PER_HEAD = C // HEADS
QUARTERS = HC // CH_PER_HEAD
QPIX = PIX // QUARTERS
SCALE = HC ** -0.5
EXPERTS, HID = 4, 4 * C
LN1_EPS, OFF_EPS, LN2_EPS = 1e-6, 1e-5, 1e-5

TP = 112
NT = PIX // TP
GRP = 4
NG = NT // GRP
GPIX = GRP * TP
SP = 98
NS = SAMPLES // SP
YPIX = QPIX // 2
NY = PIX // YPIX
HCH = 128
NCH = EXPERTS * HID // HCH
CPE = HID // HCH
TAPS = 9
PAIRS = PIX // 2
ODD_BASE = PAIRS + 1
TABLE_ROWS = ODD_BASE + PAIRS

ACT_JOBS = ([("xT", g) for g in range(NG)] + [("xc", g) for g in range(NG)]
            + [("offT", g) for g in range(2)] + [("keyT", g) for g in range(2)]
            + [("offc", g) for g in range(1)] + [("valT", g) for g in range(NG)]
            + [("mix", g) for g in range(QUARTERS)]
            + [("x1T", g) for g in range(NG)] + [("x1c", g) for g in range(NG)]
            + [("gateT", 0)])
DVE_JOBS = ([("offs", 0)] + [("kv", g) for g in range(QUARTERS)] + [("y", g) for g in range(NY)]
            + [("score", 0)])
NA, ND = len(ACT_JOBS), len(DVE_JOBS)
DVE_STEPS = 154


def build(nc, t, out):
    f32, f32r, i32 = mybir.dt.float32, mybir.dt.float32r, mybir.dt.int32
    ALU, ACT, AX = mybir.AluOpType, mybir.ActivationFunctionType, mybir.AxisListType
    table = nc.dram_tensor("value_table", (TABLE_ROWS, 2 * C), f32, kind="Internal").ap()
    gates = nc.dram_tensor("gate_rows", (NG, EXPERTS * GPIX), f32, kind="Internal").ap()
    with ExitStack() as ctx:
        def sb(name, shape, dt=f32):
            return ctx.enter_context(nc.sbuf_tensor(name, shape, dt))

        def pb(name, shape):
            return ctx.enter_context(nc.psum_tensor(name, shape, f32))

        def sem(name):
            return ctx.enter_context(nc.semaphore(name))

        ident = sb("ident", [128, 128])
        head_mask = sb("head_mask", [C, C])
        ref = sb("ref", [SP, NS, 2])
        conv_w = sb("conv_w", [C, 4, TAPS])
        conv_b = sb("conv_b", [C, 4])
        ln_gb = sb("ln_gb", [C, 2])
        woff2 = sb("woff2", [C, 2])
        wout = sb("wout", [C, C])
        gate_w = sb("gate_w", [C, EXPERTS])
        gate_b = sb("gate_b", [TP, EXPERTS])
        w1_hi = sb("w1_hi", [C, EXPERTS * HID], f32r)
        w1_lo = sb("w1_lo", [C, EXPERTS * HID], f32r)
        b1 = sb("b1", [HCH, NCH])
        w2 = sb("w2", [HCH, NCH, C])
        b2 = sb("b2", [C, EXPERTS])
        x = sb("x", [C, PIX])
        xT = sb("xT", [TP, NT, C])
        xn = sb("xn", [TP, NT, C])
        xpad = sb("xpad", [C, H + 2, W + 2])
        off = sb("off", [C, HK, WK])
        key = sb("key", [C, HK, WK])
        val = sb("val", [C, H, W])
        query = sb("query", [C, H, W])
        offT = sb("offT", [SP, NS, C])
        offn = sb("offn", [SP, NS, C])
        offg = sb("offg", [C, SAMPLES])
        keyT = sb("keyT", [SP, NS, C])
        valT = xn
        got = sb("got", [128, NS * 4 * C])
        w1 = got[0:C, 0:EXPERTS * HID]
        got = got[0:SP, :].rearrange("p (n r a c) -> p n r a c", n=NS, r=2, a=2)
        vs = sb("vs", [SP, NS, C])
        kv = sb("kv", [C, QUARTERS, QUARTERS, C])
        mix = sb("mix", [C, QUARTERS, QUARTERS, C])
        x1 = sb("x1", [C, PIX])
        st = sb("st", [128, NT, 6])
        sa = sb("sa", [128, NT])
        sd = sb("sd", [128, NT])
        sv = sb("sv", [128, NT])
        si = sb("si", [128, NT], i32)
        su = sb("su", [128, NT])
        mean = sb("mean", [128, NT])
        rstd = sb("rstd", [128, NT])
        pz = sb("pz", [SP, NS, 2])
        pt = sb("pt", [SP, NS, 2])
        pos = sb("pos", [SP, NS, 2])
        fl = sb("fl", [SP, NS, 2])
        gt = sb("gt", [SP, NS, 2])
        wf = sb("wf", [SP, NS, 2])
        wi = sb("wi", [SP, NS, 2])
        hx = sb("hx", [SP, NS])
        hg = sb("hg", [SP, NS])
        ix = sb("ix", [SP, NS])
        w4 = sb("w4", [SP, NS, 2, 2])
        rows = sb("rows", [SP, 2, NS], i32)
        sc = sb("sc", [TP, NT, EXPERTS])
        ex = sb("ex", [TP, NT, EXPERTS])
        mx = sb("mx", [TP, NT])
        rank = sb("rank", [TP, NT, EXPERTS])
        cmp = sb("cmp", [TP, NT, EXPERTS])
        gate = sb("gate", [TP, NG, EXPERTS, GRP])
        gateT = sb("gateT", [NT * EXPERTS, TP])
        xc = val[:, :, :].rearrange("c h w -> c (h w)")
        xh = sb("xh", [C, PIX], f32r)
        xl = sb("xl", [C, PIX], f32r)
        gate_all = sb("gate_all", [C, 2, EXPERTS, GPIX])
        hid = sb("hid", [HCH, 3, GPIX])
        ye = sb("ye", [C, EXPERTS, GPIX])
        res = sb("res", [C, 2, GPIX])

        pa = [pb(f"pa{i}", [128, 512]) for i in range(2)]
        pd = [pb(f"pd{i}", [128, 512]) for i in range(2)]
        ph = [pb(f"ph{i}", [128, 512]) for i in range(2)]
        py = [pb(f"py{i}", [128, 512]) for i in range(2)]

        consts_in = sem("consts_in")
        weights_split = sem("weights_split")
        x_in = sem("x_in")
        act_full = sem("act_full")
        act_done = sem("act_done")
        dve_full = sem("dve_full")
        dve_done = sem("dve_done")
        dve_step = sem("dve_step")
        x_normed = sem("x_normed")
        pad_zero = sem("pad_zero")
        off_conv = sem("off_conv")
        key_conv = sem("key_conv")
        val_conv = sem("val_conv")
        query_conv = sem("query_conv")
        off_normed = sem("off_normed")
        pos_raw = sem("pos_raw")
        pos_tanh = sem("pos_tanh")
        rows_ready = sem("rows_ready")
        table_out = sem("table_out")
        table_edge = sem("table_edge")
        gathered = sem("gathered")
        sampled = sem("sampled")
        x1_normed = sem("x1_normed")
        score_ready = sem("score_ready")
        score_exp = sem("score_exp")
        gate_ready = sem("gate_ready")
        gate_out = sem("gate_out")
        gate_in = [sem(f"gate_in{i}") for i in range(2)]
        x_split = sem("x_split")
        hid_full = sem("hid_full")
        hid_act = sem("hid_act")
        hid_used = sem("hid_used")
        ye_ready = sem("ye_ready")
        pool_step = sem("pool_step")
        res_ready = sem("res_ready")
        res_out = [sem(f"res_out{i}") for i in range(2)]

        consts = [(ident, "ident"), (head_mask, "head_mask"), (ref, "ref"), (conv_w, "conv_w"),
                  (conv_b, "conv_b"), (ln_gb, "ln_gb"), (woff2, "woff2"), (wout, "wout"),
                  (gate_w, "gate_w"), (b1, "b1"), (b2, "b2"), (w1.rearrange("c (e h) -> c e h", e=EXPERTS), "w1"), (w2, "w2")]
        NCONST = 16 * (len(consts) + 1)

        def aj(name, g=0):
            return ACT_JOBS.index((name, g)) + 1

        def dj(name, g=0):
            return DVE_JOBS.index((name, g)) + 1

        x_rows = t["x"].rearrange("b c h w -> (b c) (h w)")
        out_rows = out.rearrange("b c h w -> (b c) (h w)")
        blk = ctx.enter_context(nc.Block())

        @blk.sync
        def _(sp):
            for dst, name in consts:
                sp.dma_start(dst if name == "w1" else dst[:], t[name]).then_inc(consts_in, 16)
            sp.dma_start(gate_b[:, :], t["gate_b"].to_broadcast([TP, EXPERTS])).then_inc(consts_in, 16)
            sp.wait_ge(pad_zero, 1)
            flat = table.rearrange("r c -> (r c)")
            for start in (PIX * C, TABLE_ROWS * 2 * C - C):
                sp.dma_start(flat[start:start + C].rearrange("(c o) -> c o", o=1), xpad[:, 0, 0:1]).then_inc(table_edge, 16)
            with sp.Fori(0, BATCH) as b:
                values_at = sp.snap(b * NA + aj("valT", NG - 1))
                gates_at = sp.snap(b * NA + aj("gateT"))
                rows_at = sp.snap(b * 16 + 16)
                gated_at = [sp.snap(b * NG * EXPERTS + EXPERTS * (g + 1)) for g in range(NG - 2)]
                summed_at = [sp.snap(b * NG + g + 1) for g in range(NG)]
                image = sp.snap(b * C)
                sp.dma_start(x[:, :], x_rows[bass.ds(image, C), :]).then_inc(x_in, 16)
                sp.wait_ge(act_done, values_at)
                odd = ODD_BASE * 2 * C - C
                for start in (0, odd):
                    sp.dma_start(flat[start:start + PIX * C].rearrange("(p k) -> p k", p=TP),
                                 valT[:, :, :].rearrange("p t c -> p (t c)")).then_inc(table_out, 16)
                sp.wait_ge(act_done, gates_at)
                sp.dma_start(gates.rearrange("g (r p) -> (g r) p", p=TP), gateT[:, :]).then_inc(gate_out, 16)
                sp.wait_ge(gate_out, rows_at)
                for g in range(NG):
                    if g >= 2:
                        sp.wait_ge(ye_ready, gated_at[g - 2])
                    sp.dma_start(gate_all[:, g % 2].rearrange("c e p -> c (e p)"),
                                 gates[g:g + 1, :].to_broadcast([C, EXPERTS * GPIX])).then_inc(gate_in[g % 2], 16)
                    for m in ([g - 1] if g >= 1 else []) + ([g] if g == NG - 1 else []):
                        sp.wait_ge(res_ready, summed_at[m])
                        sp.dma_start(out_rows[bass.ds(image, C), m * GPIX:(m + 1) * GPIX], res[:, m % 2, :]).then_inc(res_out[m % 2], 16)
            sp.wait_ge(res_out[0], BATCH * 16 * ((NG + 1) // 2))
            sp.wait_ge(res_out[1], BATCH * 16 * (NG // 2))

        @blk.tensor
        def _(pe):
            def act_bank(b, name, g=0):
                j = aj(name, g) - 1
                if j >= 2:
                    pe.wait_ge(act_done, b * NA + j - 1)
                return pa[j % 2]

            def dve_bank(b, name, g=0):
                j = dj(name, g) - 1
                if j >= 2:
                    pe.wait_ge(dve_done, b * ND + j - 1)
                return pd[j % 2]

            def transposes(bank, ins, size, n):
                for k, piece in enumerate(ins):
                    last = nc.tensor.transpose(bank[0:n, k * size:(k + 1) * size], piece, ident[0:size, 0:size])
                return last

            pe.wait_ge(consts_in, NCONST)
            pe.wait_ge(weights_split, 1)
            with pe.Fori(0, BATCH) as b:
                pe.wait_ge(x_in, b * 16 + 16)
                for g in range(NG):
                    bank = act_bank(b, "xT", g)
                    transposes(bank, [x[:, (GRP * g + k) * TP:(GRP * g + k + 1) * TP] for k in range(GRP)], C, TP).then_inc(act_full, 1)
                for g in range(NG):
                    pe.wait_ge(x_normed, b * NG + g + 1)
                    bank = act_bank(b, "xc", g)
                    transposes(bank, [xn[:, GRP * g + k, :] for k in range(GRP)], TP, C).then_inc(act_full, 1)
                offf, keyf = (m[:, :, :].rearrange("c h w -> c (h w)") for m in (off, key))
                for name, src, ready in (("offT", offf, off_conv), ("keyT", keyf, key_conv)):
                    pe.wait_ge(ready, b + 1)
                    for g in range(2):
                        bank = act_bank(b, name, g)
                        transposes(bank, [src[:, (4 * g + k) * SP:(4 * g + k + 1) * SP] for k in range(4)], C, SP).then_inc(act_full, 1)
                pe.wait_ge(off_normed, b + 1)
                j = aj("offc") - 1
                pe.wait_ge(act_done, b * NA + j)
                for g in range(2):
                    last = transposes(pa[g], [offn[:, 4 * g + k, :] for k in range(4)], SP, C)
                last.then_inc(act_full, 1)
                pe.wait_ge(act_done, b * NA + aj("offc"))
                bank = dve_bank(b, "offs")
                for k in range(NS):
                    last = nc.tensor.matmul(bank[0:SP, 2 * k:2 * k + 2], offg[:, k * SP:(k + 1) * SP], woff2[:, :], start=True, stop=True)
                last.then_inc(dve_full, 1)
                pe.wait_ge(val_conv, b + 1)
                valf = val[:, :, :].rearrange("c h w -> c (h w)").rearrange("c (p t) -> c t p", t=NT)
                for g in range(NG):
                    bank = act_bank(b, "valT", g)
                    transposes(bank, [valf[:, GRP * g + k, :] for k in range(GRP)], C, TP).then_inc(act_full, 1)
                keyq = keyT[:, :, :].rearrange("p (q h) c -> p h q c", h=2)
                for q in range(QUARTERS):
                    pe.wait_ge(sampled, b * QUARTERS + q + 1)
                    bank = dve_bank(b, "kv", q)
                    for h in range(2):
                        last = nc.tensor.matmul(bank[0:C, 0:QUARTERS * C], vs[:, 2 * q + h, :], keyq[:, h], start=(h == 0), stop=(h == 1))
                    last.then_inc(dve_full, 1)
                for q in range(QUARTERS):
                    pe.wait_ge(dve_done, b * ND + dj("kv", q))
                    bank = act_bank(b, "mix", q)
                    for k in range(QUARTERS):
                        last = nc.tensor.matmul(bank[0:C, k * C:(k + 1) * C], kv[:, q, k, :], wout[:, :], start=True, stop=True)
                    last.then_inc(act_full, 1)
                pe.wait_ge(query_conv, b + 1)
                queryf = query[:, :, :].rearrange("c h w -> c (h w)")
                for n in range(NY):
                    q, h = n // 2, n % 2
                    pe.wait_ge(act_done, b * NA + aj("mix", q))
                    bank = dve_bank(b, "y", n)
                    for k in range(QUARTERS):
                        last = nc.tensor.matmul(bank[0:C, 0:YPIX], mix[:, q, k, :], queryf[:, k * QPIX + h * YPIX:k * QPIX + (h + 1) * YPIX],
                                                start=(k == 0), stop=(k == QUARTERS - 1))
                    last.then_inc(dve_full, 1)
                for g in range(NG):
                    pe.wait_ge(dve_done, b * ND + dj("y", min(NY - 1, ((g + 1) * GPIX - 1) // YPIX)))
                    bank = act_bank(b, "x1T", g)
                    transposes(bank, [x1[:, (GRP * g + k) * TP:(GRP * g + k + 1) * TP] for k in range(GRP)], C, TP).then_inc(act_full, 1)
                for g in range(NG):
                    pe.wait_ge(x1_normed, b * NG + g + 1)
                    bank = act_bank(b, "x1c", g)
                    transposes(bank, [xn[:, GRP * g + k, :] for k in range(GRP)], TP, C).then_inc(act_full, 1)
                pe.wait_ge(act_done, b * NA + aj("x1c", NG - 1))
                bank = dve_bank(b, "score")
                for k in range(NT):
                    last = nc.tensor.matmul(bank[0:TP, EXPERTS * k:EXPERTS * (k + 1)], xc[:, k * TP:(k + 1) * TP], gate_w[:, :], start=True, stop=True)
                last.then_inc(dve_full, 1)
                pe.wait_ge(gate_ready, b + 1)
                bank = act_bank(b, "gateT")
                transposes(bank, [gate[:, :, :, :].rearrange("p g e s -> p (g e s)")], TP, NT * EXPERTS).then_inc(act_full, 1)
                for g in range(NG):
                    pe.wait_ge(x_split, b * NG + g + 1)
                    px = slice(g * GPIX, (g + 1) * GPIX)

                    def second(c):
                        pe.wait_ge(hid_act, (b * NG + g) * NCH + c + 1)
                        e, j = c // CPE, c % CPE
                        if j == 0 and (g >= 1 or e >= 2):
                            pe.wait_ge(ye_ready, (b * NG + g) * EXPERTS + e - 1)
                        nc.tensor.matmul(py[e % 2][0:C, 0:GPIX], w2[:, c, :], hid[:, c % 3, :], start=(j == 0), stop=(j == CPE - 1)).then_inc(hid_used, 1)

                    for c in range(NCH):
                        if c >= 2 or g >= 1:
                            pe.wait_ge(hid_act, (b * NG + g) * NCH + c - 1)
                        cols = slice(c * HCH, (c + 1) * HCH)
                        bank = ph[c % 2][:, 0:GPIX]
                        nc.tensor.matmul(bank, w1_hi[:, cols], xh[:, px], start=True, stop=False)
                        nc.tensor.matmul(bank, w1_hi[:, cols], xl[:, px], start=False, stop=False)
                        nc.tensor.matmul(bank, w1_lo[:, cols], xh[:, px], start=False, stop=True).then_inc(hid_full, 1)
                        if c >= 1:
                            second(c - 1)
                    second(NCH - 1)

        @blk.scalar
        def _(act):
            def empty(b, name, g, dst, n, size, scale=1.0, func=ACT.Copy):
                j = aj(name, g) - 1
                act.wait_ge(act_full, b * NA + j + 1)
                src = pa[j % 2][0:n, 0:size]
                if len(dst.shape) == 3:
                    src = src.rearrange("p (a c) -> p a c", a=dst.shape[1])
                nc.scalar.activation(dst, src, func, scale=scale).then_inc(act_done, 1)

            act.wait_ge(pad_zero, 1)
            act.wait_ge(consts_in, NCONST)
            with act.Fori(0, BATCH) as b:
                for g in range(NG):
                    empty(b, "xT", g, xT[:, GRP * g:GRP * (g + 1), :], TP, GRP * C)
                for g in range(NG):
                    r = g * GPIX // W
                    empty(b, "xc", g, xpad[:, 1 + r:1 + r + GPIX // W, 1:1 + W], C, GPIX)
                for g in range(2):
                    empty(b, "offT", g, offT[:, 4 * g:4 * g + 4, :], SP, 4 * C)
                for g in range(2):
                    empty(b, "keyT", g, keyT[:, 4 * g:4 * g + 4, :], SP, 4 * C, scale=SCALE)
                act.wait_ge(act_full, b * NA + aj("offc"))
                half = SAMPLES // 2
                nc.scalar.activation(offg[:, 0:half], pa[0][0:C, 0:half], ACT.Gelu, bias=ln_gb[:, 1:2], scale=ln_gb[:, 0:1])
                nc.scalar.activation(offg[:, half:], pa[1][0:C, 0:half], ACT.Gelu, bias=ln_gb[:, 1:2], scale=ln_gb[:, 0:1]).then_inc(act_done, 1)
                act.wait_ge(pos_raw, b + 1)
                nc.scalar.activation(pt[:, :, :], pz[:, :, :], ACT.Tanh).then_inc(pos_tanh, 1)
                for g in range(NG):
                    empty(b, "valT", g, valT[:, GRP * g:GRP * (g + 1), :], TP, GRP * C)
                for q in range(QUARTERS):
                    empty(b, "mix", q, mix[:, q, :, :], C, QUARTERS * C)
                for g in range(NG):
                    empty(b, "x1T", g, xT[:, GRP * g:GRP * (g + 1), :], TP, GRP * C)
                for g in range(NG):
                    empty(b, "x1c", g, xc[:, g * GPIX:(g + 1) * GPIX], C, GPIX)
                act.wait_ge(score_ready, b + 1)
                nc.scalar.activation(ex[:, :, :], sc[:, :, :], ACT.Exp).then_inc(score_exp, 1)
                empty(b, "gateT", 0, gateT[:, :], NT * EXPERTS, TP)
                for g in range(NG):
                    for c in range(NCH):
                        act.wait_ge(hid_full, (b * NG + g) * NCH + c + 1)
                        if c >= 3 or g >= 1:
                            act.wait_ge(hid_used, (b * NG + g) * NCH + c - 2)
                        nc.scalar.activation(hid[:, c % 3, :], ph[c % 2][:, 0:GPIX], ACT.Gelu, bias=b1[:, c:c + 1]).then_inc(hid_act, 1)

        @blk.vector
        def _(dve):
            v = nc.vector
            n = [0]

            def step(ins):
                n[0] += 1
                ins.then_inc(dve_step, 1)
                return n[0]

            nc.vector.memset(xpad[:], 0.0).then_inc(pad_zero, 1)
            dve.wait_ge(consts_in, NCONST)
            w1f = w1
            v.tensor_copy(w1_hi[:, :], w1f).then_inc(dve_step, 1)
            dve.wait_ge(dve_step, 1)
            v.tensor_tensor(w1_lo[:, :], w1f, w1_hi[:, :].bitcast(f32), ALU.subtract).then_inc(weights_split, 1)
            BASE = 1

            with dve.Fori(0, BATCH) as b:
                def need(count):
                    dve.wait_ge(dve_step, b * DVE_STEPS + BASE + count)

                def link(ins):
                    need(step(ins))

                def statistics(np_, nt, eps):
                    S = lambda k: st[0:np_, 0:nt, k]
                    A = lambda m: m[0:np_, 0:nt]
                    step(v.tensor_tensor(A(sa), S(1), S(4), ALU.add))
                    step(v.tensor_tensor(A(sd), S(1), S(4), ALU.subtract))
                    link(v.tensor_tensor(A(sv), S(2), S(5), ALU.add))
                    step(v.tensor_scalar(A(mean), A(sa), 0.5, None, ALU.mult))
                    step(v.tensor_tensor(A(sd), A(sd), A(sd), ALU.mult))
                    link(v.tensor_scalar(A(sv), A(sv), 1.0 / C, eps, ALU.mult, ALU.add))
                    link(v.scalar_tensor_tensor(A(sv), A(sd), 0.25, A(sv), ALU.mult, ALU.add))
                    link(v.tensor_scalar(A(si), A(sv).bitcast(i32), 1, None, ALU.logical_shift_right))
                    link(v.tensor_scalar(A(rstd).bitcast(i32), A(si), -1.0, float(0x5F3759DF), ALU.mult, ALU.add))
                    for _ in range(3):
                        link(v.scalar_tensor_tensor(A(su), A(sv), -0.5, A(rstd), ALU.mult, ALU.mult))
                        link(v.tensor_tensor(A(su), A(su), A(rstd), ALU.mult))
                        link(v.scalar_tensor_tensor(A(rstd), A(su), 1.5, A(rstd), ALU.add, ALU.mult))

                def norm_tokens(name, eps, normed):
                    for g in range(NG):
                        dve.wait_ge(act_done, b * NA + aj(name, g))
                        for k in range(GRP * g, GRP * (g + 1)):
                            last = v.bn_stats(st[0:TP, k, :], xT[:, k, :])
                    link(last)
                    statistics(TP, NT, eps)
                    for k in range(NT):
                        last = v.tensor_scalar(xn[:, k, :], xT[:, k, :], mean[0:TP, k:k + 1], rstd[0:TP, k:k + 1], ALU.subtract, ALU.mult)
                        if k % GRP == GRP - 1:
                            last.then_inc(normed, 1)

                def conv(i, dst, stride, ready):
                    for tap in range(TAPS):
                        dy, dx = tap // 3, tap % 3
                        src = xpad[:, dy:dy + H:stride, dx:dx + W:stride]
                        if tap == 0:
                            link(v.tensor_scalar(dst[:, :, :], src, conv_w[:, i, 0:1], conv_b[:, i:i + 1], ALU.mult, ALU.add))
                        elif tap < TAPS - 1:
                            link(v.scalar_tensor_tensor(dst[:, :, :], src, conv_w[:, i, tap:tap + 1], dst[:, :, :], ALU.mult, ALU.add))
                        else:
                            v.scalar_tensor_tensor(dst[:, :, :], src, conv_w[:, i, tap:tap + 1], dst[:, :, :], ALU.mult, ALU.add).then_inc(ready, 1)

                def floor(dst, src, big, m=1.0):
                    link(v.tensor_scalar(dst, src, m, 8388608.0, ALU.mult, ALU.add))
                    link(v.tensor_scalar(dst, dst, 8388608.0, None, ALU.subtract))
                    link(v.scalar_tensor_tensor(big, src, m, dst, ALU.mult, ALU.is_lt))
                    link(v.tensor_tensor(dst, dst, big, ALU.subtract))

                n[0] = 0
                norm_tokens("xT", LN1_EPS, x_normed)
                dve.wait_ge(act_done, b * NA + aj("xc", NG - 1))
                conv(0, off, 2, off_conv)
                conv(1, key, 2, key_conv)
                for g in range(2):
                    dve.wait_ge(act_done, b * NA + aj("offT", g))
                    for k in range(4 * g, 4 * g + 4):
                        last = v.bn_stats(st[0:SP, k, :], offT[:, k, :])
                link(last)
                statistics(SP, NS, OFF_EPS)
                for k in range(NS):
                    last = v.tensor_scalar(offn[:, k, :], offT[:, k, :], mean[0:SP, k:k + 1], rstd[0:SP, k:k + 1], ALU.subtract, ALU.mult)
                last.then_inc(off_normed, 1)
                conv(2, val, 1, val_conv)
                dve.wait_ge(dve_full, b * ND + dj("offs"))
                v.tensor_tensor(pz[:, :, :], pd[0][0:SP, 0:2 * NS].rearrange("p (n k) -> p n k", k=2), ref[:, :, :], ALU.add).then_inc(dve_done, 1)
                dve.wait_ge(dve_done, b * ND + dj("offs"))
                v.tensor_copy(gt[:, :, :], pz[:, :, :]).then_inc(pos_raw, 1)
                dve.wait_ge(pos_tanh, b + 1)
                link(v.tensor_scalar(pos[:, :, :], pt[:, :, :], 1.0, 0.5 * (W - 1), ALU.add, ALU.mult))
                floor(fl[:, :, :], pos[:, :, :], gt[:, :, :])
                link(v.tensor_scalar(fl[:, :, :], fl[:, :, :], float(W - 2), None, ALU.min))
                step(v.tensor_tensor(wf[:, :, :], pos[:, :, :], fl[:, :, :], ALU.subtract))
                floor(hx[:, :], fl[:, :, 1], hg[:, :], 0.5)
                link(v.tensor_scalar(ix[:, :], fl[:, :, 1], float(ODD_BASE), None, ALU.mult))
                link(v.scalar_tensor_tensor(ix[:, :], hx[:, :], 1.0 - 2.0 * ODD_BASE, ix[:, :], ALU.mult, ALU.add))
                link(v.scalar_tensor_tensor(ix[:, :], fl[:, :, 0], float(W // 2), ix[:, :], ALU.mult, ALU.add))
                v.tensor_copy(rows[:, 0, :], ix[:, :])
                v.tensor_scalar(rows[:, 1, :], ix[:, :], float(W // 2), None, ALU.add).then_inc(rows_ready, 1)
                link(v.tensor_scalar(wi[:, :, :], wf[:, :, :], -1.0, 1.0, ALU.mult, ALU.add))
                for r, a in enumerate((wi, wf)):
                    for c, d in enumerate((wi, wf)):
                        last = v.tensor_tensor(w4[:, :, r, c], a[:, :, 0], d[:, :, 1], ALU.mult)
                link(last)
                conv(3, query, 1, query_conv)
                dve.wait_ge(gathered, (b + 1) * 16 * 2 * NS)
                counts = {}
                for r in range(2):
                    for c in range(2):
                        for k in range(NS):
                            w = w4[:, k, r, c:c + 1]
                            if r == c == 0:
                                counts[k] = step(v.tensor_scalar(vs[:, k, :], got[:, k, r, c, :], w, None, ALU.mult))
                                continue
                            need(counts[k])
                            ins = v.scalar_tensor_tensor(vs[:, k, :], got[:, k, r, c, :], w, vs[:, k, :], ALU.mult, ALU.add)
                            if (r, c) != (1, 1):
                                counts[k] = step(ins)
                            elif k % 2:
                                ins.then_inc(sampled, 1)
                for q in range(QUARTERS):
                    dve.wait_ge(dve_full, b * ND + dj("kv", q))
                    v.tensor_tensor(kv[:, q, :, :], pd[(dj("kv", q) - 1) % 2][0:C, 0:QUARTERS * C].rearrange("c (k d) -> c k d", d=C),
                                    head_mask[:, :].rearrange("c (o d) -> c o d", o=1).to_broadcast([C, QUARTERS, C]), ALU.mult).then_inc(dve_done, 1)
                for m in range(NY):
                    dve.wait_ge(dve_full, b * ND + dj("y", m))
                    px = slice(m * YPIX, (m + 1) * YPIX)
                    v.tensor_tensor(x1[:, px], pd[(dj("y", m) - 1) % 2][0:C, 0:YPIX], x[:, px], ALU.add).then_inc(dve_done, 1)
                norm_tokens("x1T", LN2_EPS, x1_normed)
                for g in range(NG):
                    dve.wait_ge(act_done, b * NA + aj("x1c", g))
                    px = slice(g * GPIX, (g + 1) * GPIX)
                    link(v.tensor_copy(xh[:, px], xc[:, px]))
                    v.tensor_tensor(xl[:, px], xc[:, px], xh[:, px].bitcast(f32), ALU.subtract).then_inc(x_split, 1)
                dve.wait_ge(dve_full, b * ND + dj("score"))
                full = lambda m: m[:, :].rearrange("p (t o) -> p t o", o=1).to_broadcast([TP, NT, EXPERTS])
                v.tensor_tensor(sc[:, :, :], pd[(dj("score") - 1) % 2][0:TP, 0:NT * EXPERTS].rearrange("p (t e) -> p t e", e=EXPERTS),
                                gate_b[:, :].rearrange("p (o e) -> p o e", o=1).to_broadcast([TP, NT, EXPERTS]), ALU.add).then_inc(dve_done, 1)
                dve.wait_ge(dve_done, b * ND + dj("score"))
                link(v.tensor_reduce(mx[:, :], sc[:, :, :], AX.X, ALU.max))
                v.tensor_tensor(sc[:, :, :], sc[:, :, :], full(mx), ALU.subtract).then_inc(score_ready, 1)
                dve.wait_ge(score_exp, b + 1)
                link(v.tensor_reduce(mx[:, :], ex[:, :, :], AX.X, ALU.add))
                link(v.reciprocal(mx[:, :], mx[:, :]))
                link(v.tensor_tensor(ex[:, :, :], ex[:, :, :], full(mx), ALU.mult))
                for e in range(EXPERTS):
                    last = v.memset(rank[:, :, e], float(e))
                link(last)
                for d in range(1, EXPERTS):
                    m = EXPERTS - d
                    link(v.tensor_tensor(cmp[:, :, 0:m], ex[:, :, d:], ex[:, :, 0:m], ALU.is_gt))
                    link(v.tensor_tensor(rank[:, :, 0:m], rank[:, :, 0:m], cmp[:, :, 0:m], ALU.add))
                    link(v.tensor_tensor(rank[:, :, d:], rank[:, :, d:], cmp[:, :, 0:m], ALU.subtract))
                link(v.scalar_tensor_tensor(ex[:, :, :], rank[:, :, :], 1.5, ex[:, :, :], ALU.is_lt, ALU.mult))
                link(v.tensor_reduce(mx[:, :], ex[:, :, :], AX.X, ALU.add))
                link(v.tensor_scalar(mx[:, :], mx[:, :], 1e-9, None, ALU.add))
                link(v.reciprocal(mx[:, :], mx[:, :]))
                v.tensor_tensor(gate[:, :, :, :].rearrange("p g e s -> p g s e"), ex[:, :, :].rearrange("p (g s) e -> p g s e", s=GRP),
                                mx[:, :].rearrange("p (g s o) -> p g s o", s=GRP, o=1).to_broadcast([TP, NG, GRP, EXPERTS]), ALU.mult).then_inc(gate_ready, 1)
                for g in range(NG):
                    for e in range(EXPERTS):
                        dve.wait_ge(hid_used, (b * NG + g) * NCH + (e + 1) * CPE)
                        if e == 0:
                            k = (g // 2 + 1) + 0
                            per = (NG + 1) // 2 if g % 2 == 0 else NG // 2
                            dve.wait_ge(gate_in[g % 2], (b * per + k) * 16)
                            if g >= 1:
                                dve.wait_ge(res_ready, b * NG + g)
                        v.scalar_tensor_tensor(ye[:, e, :], py[e % 2][0:C, 0:GPIX], b2[:, e:e + 1], gate_all[:, g % 2, e, :], ALU.add, ALU.mult).then_inc(ye_ready, 1)
                assert n[0] == DVE_STEPS, n[0]

        @blk.gpsimd
        def _(pool):
            p = nc.gpsimd
            steps = 0
            pool.wait_ge(table_edge, 32)
            for b in range(BATCH):
                pool.wait_ge(rows_ready, b + 1)
                pool.wait_ge(table_out, 32 * (b + 1))
                for k in range(NS):
                    for r in range(2):
                        p.indirect_dma_start(got[:, k, r, :, :].rearrange("p a c -> p (a c)"), None, table,
                                             bass.IndirectOffsetOnAxis(ap=rows[:, r, k:k + 1], axis=0)).then_inc(gathered, 16)
                for g in range(NG):
                    i = b * NG + g
                    pool.wait_ge(ye_ready, i * EXPERTS + 1)
                    per, k = ((NG + 1) // 2, g // 2) if g % 2 == 0 else (NG // 2, g // 2)
                    if b * per + k > 0:
                        pool.wait_ge(res_out[g % 2], 16 * (b * per + k))
                    r = res[:, g % 2, :]
                    for e in range(EXPERTS):
                        pool.wait_ge(ye_ready, i * EXPERTS + e + 1)
                        ins = p.tensor_tensor(r, x1[:, g * GPIX:(g + 1) * GPIX] if e == 0 else r, ye[:, e, :], ALU.add)
                        if e < EXPERTS - 1:
                            steps += 1
                            ins.then_inc(pool_step, 1)
                            pool.wait_ge(pool_step, steps)
                        else:
                            ins.then_inc(res_ready, 1)


def kernel(**inputs):
    import numpy as np
    import concourse.bacc as bacc
    from concourse.bass_utils import run_bass_kernel_spmd as run

    f = np.float32
    a = {k: np.asarray(v) for k, v in inputs.items()}
    conv = [("off1"), ("k"), ("v"), ("q")]
    n = np.arange(SAMPLES).reshape(NS, SP).T
    ref = np.stack([(n // WK + 0.5).astype(f) / f(HK) * f(2) - f(1), (n % WK + 0.5).astype(f) / f(WK) * f(2) - f(1)], axis=-1)
    ch = np.arange(C) // CH_PER_HEAD
    arrays = {
        "x": a["x"],
        "ident": np.eye(128, dtype=f),
        "head_mask": (ch[:, None] == ch[None, :]).astype(f),
        "ref": ref.astype(f),
        "conv_w": np.stack([a[f"L0_conv_w_{k}"].reshape(C, TAPS) for k in conv], axis=1),
        "conv_b": np.stack([a[f"L0_conv_b_{k}"] for k in conv], axis=1),
        "ln_gb": np.stack([a["L0_conv_ln_g"], a["L0_conv_ln_b"]], axis=1),
        "woff2": a["L0_conv_w_off2"].T,
        "wout": a["L0_conv_w_out"].T,
        "gate_w": a["L0_ffn_gate_w"],
        "gate_b": a["L0_ffn_gate_b"].reshape(1, EXPERTS),
        "w1": a["L0_ffn_w1"].transpose(1, 0, 2),
        "b1": a["L0_ffn_b1"].reshape(NCH, HCH).T,
        "w2": a["L0_ffn_w2"].reshape(NCH, HCH, C).transpose(1, 0, 2),
        "b2": a["L0_ffn_b2"].T,
    }
    arrays = {"in_" + k: np.ascontiguousarray(v) for k, v in arrays.items()}
    nc = bacc.Bacc("TRN2", target_bir_lowering=False, num_devices=1)
    t = {k[3:]: nc.dram_tensor(k, v.shape, mybir.dt.from_np(v.dtype), kind="ExternalInput").ap() for k, v in arrays.items()}
    out = nc.dram_tensor("out", (BATCH, C, H, W), mybir.dt.float32, kind="ExternalOutput").ap()
    build(nc, t, out)
    r = run(nc, [arrays], core_ids=[0])
    return r.results[0]["out"]
```

```python
import concourse.bass as bass
from concourse import mybir
from contextlib import ExitStack

BATCH, C, H, W = 4, 96, 56, 56
PIX = H * W
HK, WK = H // 2, W // 2
SAMPLES = HK * WK
HEADS, HC = 12, 32
CH_PER_HEAD = C // HEADS
QUARTERS = HC // CH_PER_HEAD
QPIX = PIX // QUARTERS
SCALE = HC ** -0.5
EXPERTS, HID = 4, 4 * C
LN1_EPS, OFF_EPS, LN2_EPS = 1e-6, 1e-5, 1e-5

TP = 112
NT = PIX // TP
GRP = 4
NG = NT // GRP
GPIX = GRP * TP
SP = 98
NS = SAMPLES // SP
YPIX = QPIX // 2
NY = PIX // YPIX
HCH = 128
NCH = EXPERTS * HID // HCH
CPE = HID // HCH
TAPS = 9
PAIRS = PIX // 2
ODD_BASE = PAIRS + 1
TABLE_ROWS = ODD_BASE + PAIRS

ACT_JOBS = ([("xT", g) for g in range(NG)] + [("xc", g) for g in range(NG)]
            + [("offT", g) for g in range(2)] + [("keyT", g) for g in range(2)]
            + [("offc", g) for g in range(2)] + [("valT", g) for g in range(NG)]
            + [("mix", g) for g in range(QUARTERS)]
            + [("x1T", g) for g in range(NG)] + [("x1c", g) for g in range(NG)]
            + [("gateT", 0)])
DVE_JOBS = ([("offs", 0)] + [("kv", g) for g in range(QUARTERS)] + [("y", g) for g in range(NY)]
            + [("score", 0)])
NA, ND = len(ACT_JOBS), len(DVE_JOBS)
DVE_STEPS = 154
CHUNKS = NG * NCH
OUTPUTS = NG * EXPERTS
OUTPUT_EVERY = 4.2
OUTPUT_LAG = 6.0
WAITED = ["xc", "offT", "keyT", "offc", "tanh", "valT", "y", "kv", "x1T", "x1c", "score", "gateT", "gateT"]
FREE_OUTPUTS = EXPERTS
NORM_DVE = 4

AT = {"xT": 0, "xc": 7, "offT": 13, "keyT": 19, "offc": 22, "offs": 24, "tanh": 32, "valT": 46,
      "kv": 74, "mix": 74, "y": 75, "x1T": 77, "x1c": 80, "score": 83, "gateT": 84}



def build(nc, t, out):
    f32, f32r, i32 = mybir.dt.float32, mybir.dt.float32r, mybir.dt.int32
    ALU, ACT, AX = mybir.AluOpType, mybir.ActivationFunctionType, mybir.AxisListType
    table = nc.dram_tensor("value_table", (TABLE_ROWS, 2 * C), f32, kind="Internal").ap()
    gates = nc.dram_tensor("gate_rows", (BATCH * NG, EXPERTS * GPIX), f32, kind="Internal").ap()
    with ExitStack() as ctx:
        def sb(name, shape, dt=f32):
            return ctx.enter_context(nc.sbuf_tensor(name, shape, dt))

        def pb(name, shape):
            return ctx.enter_context(nc.psum_tensor(name, shape, f32))

        def sem(name):
            return ctx.enter_context(nc.semaphore(name))

        ident = sb("ident", [128, 128])
        head_mask = sb("head_mask", [C, C])
        ref = sb("ref", [SP, NS, 2])
        conv_w = sb("conv_w", [C, 4, TAPS])
        conv_b = sb("conv_b", [C, 4])
        ln_gb = sb("ln_gb", [C, 2])
        woff2 = sb("woff2", [C, 2])
        wout = sb("wout", [C, C])
        gate_w = sb("gate_w", [C, EXPERTS])
        gate_b = sb("gate_b", [TP, EXPERTS])
        w1_hi = sb("w1_hi", [C, EXPERTS * HID], f32r)
        w1_lo = sb("w1_lo", [C, EXPERTS * HID], f32r)
        b1 = sb("b1", [HCH, NCH])
        w2 = sb("w2", [HCH, NCH, C])
        b2 = sb("b2", [C, EXPERTS])
        x = sb("x", [C, PIX])
        xT = sb("xT", [TP, NT, C])
        valT = xT
        xpad = sb("xpad", [C, H + 2, W + 2])
        big = sb("big", [128, PIX])
        w1 = big[0:C, 0:EXPERTS * HID]
        val = big[0:C, :].rearrange("c (h w) -> c h w", h=H)
        got = big[0:SP, 0:NS * 4 * C].rearrange("p (n r a c) -> p n r a c", n=NS, r=2, a=2)
        xc = big[0:C, :]
        query = sb("query", [C, H, W])
        key = sb("key", [C, HK, WK])
        keyT = sb("keyT", [SP, NS, C])
        vs = sb("vs", [SP, NS, C])
        off_area = sb("off_area", [128, 2, 2 * SAMPLES])
        off = off_area[0:C, 0, 0:SAMPLES].rearrange("c (h w) -> c h w", h=HK)
        offT = off_area[0:SP, 0, SAMPLES:SAMPLES + NS * C].rearrange("p (n c) -> p n c", n=NS)
        offg = off_area[0:C, 1, 0:SAMPLES]
        kv = off_area[0:C, 0, 0:QUARTERS * QUARTERS * C].rearrange("c (q k d) -> c q k d", q=QUARTERS, k=QUARTERS)
        mix = off_area[0:C, 1, 0:QUARTERS * QUARTERS * C].rearrange("c (q k d) -> c q k d", q=QUARTERS, k=QUARTERS)
        st = sb("st", [128, NT, 6])
        sa = sb("sa", [128, NT])
        sd = sb("sd", [128, NT])
        sv = sb("sv", [128, NT])
        si = sb("si", [128, NT], i32)
        su = sb("su", [128, NT])
        mean = sb("mean", [128, NT])
        rstd = sb("rstd", [128, NT])
        shift = sb("shift", [128, NT])
        pz = sb("pz", [SP, NS, 2])
        pt = sb("pt", [SP, NS, 2])
        pos = sb("pos", [SP, NS, 2])
        fl = sb("fl", [SP, NS, 2])
        gt = sb("gt", [SP, NS, 2])
        wf = sb("wf", [SP, NS, 2])
        wi = sb("wi", [SP, NS, 2])
        hx = sb("hx", [SP, NS])
        hg = sb("hg", [SP, NS])
        ix = sb("ix", [SP, NS])
        w4 = sb("w4", [SP, NS, 2, 2])
        rows = sb("rows", [SP, 2, NS], i32)
        sc = sb("sc", [TP, NT, EXPERTS])
        ex = sb("ex", [TP, NT, EXPERTS])
        mx = sb("mx", [TP, NT])
        rank = sb("rank", [TP, NT, EXPERTS])
        cmp = sb("cmp", [TP, NT, EXPERTS])
        gate = sb("gate", [TP, NG, EXPERTS, GRP])
        gateT = sb("gateT", [NT * EXPERTS, TP])
        x1 = sb("x1", [C, 2, PIX])
        xh = sb("xh", [C, 2 * PIX], f32r)
        xl = sb("xl", [C, 2 * PIX], f32r)
        gate_all = sb("gate_all", [C, EXPERTS, GPIX])
        hid = sb("hid", [HCH, 3, GPIX])
        ye = sb("ye", [C, EXPERTS, GPIX])
        res = sb("res", [C, 2, GPIX])

        pa = [pb(f"pa{i}", [128, 512]) for i in range(2)]
        pd = [pb(f"pd{i}", [128, 512]) for i in range(2)]
        ph = [pb(f"ph{i}", [128, 512]) for i in range(2)]
        py = [pb(f"py{i}", [128, 512]) for i in range(2)]

        consts_in = sem("consts_in")
        weights_split = sem("weights_split")
        x_in = sem("x_in")
        act_full = sem("act_full")
        act_done = sem("act_done")
        dve_full = sem("dve_full")
        dve_done = sem("dve_done")
        dve_step = sem("dve_step")
        x_stats = sem("x_stats")
        x_normed = sem("x_normed")
        x_normed_act = sem("x_normed_act")
        pad_zero = sem("pad_zero")
        off_conv = sem("off_conv")
        key_conv = sem("key_conv")
        val_conv = sem("val_conv")
        query_conv = sem("query_conv")
        off_normed = sem("off_normed")
        pos_raw = sem("pos_raw")
        pos_tanh = sem("pos_tanh")
        rows_ready = sem("rows_ready")
        table_out = sem("table_out")
        table_edge = sem("table_edge")
        gathered = sem("gathered")
        sampled = sem("sampled")
        x1_stats = sem("x1_stats")
        x1_normed = sem("x1_normed")
        x1_normed_act = sem("x1_normed_act")
        x1_kept = sem("x1_kept")
        score_ready = sem("score_ready")
        score_exp = sem("score_exp")
        gate_ready = sem("gate_ready")
        gate_out = sem("gate_out")
        gate_in = [sem(f"gate_in{i}") for i in range(2)]
        x_split = sem("x_split")
        hid_full = sem("hid_full")
        hid_act = sem("hid_act")
        hid_used = sem("hid_used")
        ye_ready = sem("ye_ready")
        ye_summed = sem("ye_summed")
        res_out = [sem(f"res_out{i}") for i in range(2)]

        consts = [(ident, "ident"), (head_mask, "head_mask"), (ref, "ref"), (conv_w, "conv_w"),
                  (conv_b, "conv_b"), (ln_gb, "ln_gb"), (woff2, "woff2"), (wout, "wout"),
                  (gate_w, "gate_w"), (b1, "b1"), (b2, "b2"), (w1.rearrange("c (e h) -> c e h", e=EXPERTS), "w1"), (w2, "w2")]
        NCONST = 16 * (len(consts) + 1)

        def aj(name, g=0):
            return ACT_JOBS.index((name, g)) + 1

        def dj(name, g=0):
            return DVE_JOBS.index((name, g)) + 1

        flat = table.rearrange("r c -> (r c)")
        x_rows = t["x"].rearrange("b c h w -> (b c) (h w)")
        out_rows = out.rearrange("b c h w -> (b c) (h w)")

        def wait(eng, semaphore, value):
            if not (isinstance(value, int) and value <= 0):
                eng.wait_ge(semaphore, value)

        def half(b):
            return (b % 2) * PIX

        blk = ctx.enter_context(nc.Block())

        @blk.sync
        def _(sp):
            for dst, name in consts:
                sp.dma_start(dst if name == "w1" else dst[:], t[name]).then_inc(consts_in, 16)
            sp.dma_start(gate_b[:, :], t["gate_b"].to_broadcast([TP, EXPERTS])).then_inc(consts_in, 16)
            sp.wait_ge(pad_zero, 1)
            for start in (PIX * C, TABLE_ROWS * 2 * C - C):
                sp.dma_start(flat[start:start + C].rearrange("(c o) -> c o", o=1), xpad[:, 0, 0:1]).then_inc(table_edge, 16)

            def load_x(b):
                wait(sp, x1_kept, 16 * b)
                wait(sp, act_done, (b - 1) * NA + aj("x1T", NG - 1) if b else 0)
                sp.dma_start(x[:, :], x_rows[b * C:(b + 1) * C, :]).then_inc(x_in, 16)

            def keep_x1(b):
                sp.wait_ge(dve_done, b * ND + dj("y", NY - 1))
                sp.dma_start(x1[:, b % 2, :], x[:, :]).then_inc(x1_kept, 16)

            def store_gates(b):
                sp.wait_ge(act_done, b * NA + aj("gateT"))
                sp.dma_start(gates[b * NG:(b + 1) * NG, :].rearrange("g (r p) -> (g r) p", p=TP), gateT[:, :]).then_inc(gate_out, 16)

            def load_gates(b, g):
                if g == 0:
                    sp.wait_ge(gate_out, 16 * (b + 1))
                for k in range(2):
                    sp.wait_ge(ye_ready, FREE_OUTPUTS + b * OUTPUTS + EXPERTS * (g - 1) + 2 * k + 2)
                    sp.dma_start(gate_all[:, 2 * k:2 * k + 2, :].rearrange("c e p -> c (e p)"),
                                 gates[b * NG + g:b * NG + g + 1, 2 * k * GPIX:(2 * k + 2) * GPIX].to_broadcast([C, 2 * GPIX])).then_inc(gate_in[k], 16)

            def store_result(b, g):
                sp.wait_ge(ye_summed, EXPERTS + b * OUTPUTS + EXPERTS * (g + 1))
                sp.dma_start(out_rows[b * C:(b + 1) * C, g * GPIX:(g + 1) * GPIX], res[:, g % 2, :]).then_inc(res_out[g % 2], 16)

            load_x(0)
            keep_x1(0)
            load_x(1)
            store_gates(0)
            for b in range(BATCH):
                load_gates(b, 0)
                for g in range(NG):
                    if g < NG - 1:
                        load_gates(b, g + 1)
                    store_result(b, g)
                if b < BATCH - 1:
                    keep_x1(b + 1)
                if b < BATCH - 2:
                    load_x(b + 2)
                if b < BATCH - 1:
                    store_gates(b + 1)
            sp.wait_ge(res_out[0], BATCH * 16 * ((NG + 1) // 2))
            sp.wait_ge(res_out[1], BATCH * 16 * (NG // 2))

        @blk.tensor
        def _(pe):
            def act_bank(b, name, g=0):
                j = aj(name, g) - 1
                wait(pe, act_done, b * NA + j - 1)
                return pa[j % 2]

            def dve_bank(b, name, g=0):
                j = dj(name, g) - 1
                wait(pe, dve_done, b * ND + j - 1)
                return pd[j % 2]

            def transposes(bank, ins, size, n):
                for k, piece in enumerate(ins):
                    last = nc.tensor.transpose(bank[0:n, k * size:(k + 1) * size], piece, ident[0:size, 0:size])
                return last

            def channels_back(b, name, normed, normed_act):
                for g in range(NG):
                    if g < NORM_DVE:
                        pe.wait_ge(normed, b * NORM_DVE + g + 1)
                    else:
                        pe.wait_ge(normed_act, b * (NG - NORM_DVE) + g - NORM_DVE + 1)
                    bank = act_bank(b, name, g)
                    transposes(bank, [xT[:, GRP * g + k, :] for k in range(GRP)], TP, C).then_inc(act_full, 1)

            def attention(b, experts_to):
                experts_to(AT["xT"])
                pe.wait_ge(x_in, b * 16 + 16)
                for g in range(NG):
                    bank = act_bank(b, "xT", g)
                    transposes(bank, [x[:, (GRP * g + k) * TP:(GRP * g + k + 1) * TP] for k in range(GRP)], C, TP).then_inc(act_full, 1)
                experts_to(AT["xc"])
                channels_back(b, "xc", x_normed, x_normed_act)
                offf, keyf = (m.rearrange("c h w -> c (h w)") for m in (off, key[:, :, :]))
                for name, src, ready in (("offT", offf, off_conv), ("keyT", keyf, key_conv)):
                    experts_to(AT[name])
                    pe.wait_ge(ready, b + 1)
                    for g in range(2):
                        bank = act_bank(b, name, g)
                        transposes(bank, [src[:, (4 * g + k) * SP:(4 * g + k + 1) * SP] for k in range(4)], C, SP).then_inc(act_full, 1)
                experts_to(AT["offc"])
                pe.wait_ge(off_normed, b + 1)
                for g in range(2):
                    bank = act_bank(b, "offc", g)
                    transposes(bank, [offT[:, 4 * g + k, :] for k in range(4)], SP, C).then_inc(act_full, 1)
                experts_to(AT["offs"])
                pe.wait_ge(act_done, b * NA + aj("offc", 1))
                bank = dve_bank(b, "offs")
                for k in range(NS):
                    last = nc.tensor.matmul(bank[0:SP, 2 * k:2 * k + 2], offg[:, k * SP:(k + 1) * SP], woff2[:, :], start=True, stop=True)
                last.then_inc(dve_full, 1)
                experts_to(AT["valT"])
                pe.wait_ge(val_conv, b + 1)
                valf = val.rearrange("c h w -> c (h w)").rearrange("c (p t) -> c t p", t=NT)
                for g in range(NG):
                    bank = act_bank(b, "valT", g)
                    transposes(bank, [valf[:, GRP * g + k, :] for k in range(GRP)], C, TP).then_inc(act_full, 1)
                experts_to(AT["kv"])
                keyq = keyT[:, :, :].rearrange("p (q h) c -> p h q c", h=2)
                for q in range(QUARTERS):
                    pe.wait_ge(sampled, b * QUARTERS + q + 1)
                    bank = dve_bank(b, "kv", q)
                    for h in range(2):
                        last = nc.tensor.matmul(bank[0:C, 0:QUARTERS * C], vs[:, 2 * q + h, :], keyq[:, h], start=(h == 0), stop=(h == 1))
                    last.then_inc(dve_full, 1)
                experts_to(AT["mix"])
                for q in range(QUARTERS):
                    pe.wait_ge(dve_done, b * ND + dj("kv", q))
                    bank = act_bank(b, "mix", q)
                    for k in range(QUARTERS):
                        last = nc.tensor.matmul(bank[0:C, k * C:(k + 1) * C], kv[:, q, k, :], wout[:, :], start=True, stop=True)
                    last.then_inc(act_full, 1)
                experts_to(AT["y"])
                pe.wait_ge(query_conv, b + 1)
                queryf = query[:, :, :].rearrange("c h w -> c (h w)")
                for n in range(NY):
                    q, h = n // 2, n % 2
                    pe.wait_ge(act_done, b * NA + aj("mix", q))
                    bank = dve_bank(b, "y", n)
                    for k in range(QUARTERS):
                        last = nc.tensor.matmul(bank[0:C, 0:YPIX], mix[:, q, k, :], queryf[:, k * QPIX + h * YPIX:k * QPIX + (h + 1) * YPIX],
                                                start=(k == 0), stop=(k == QUARTERS - 1))
                    last.then_inc(dve_full, 1)
                experts_to(AT["x1T"])
                for g in range(NG):
                    pe.wait_ge(dve_done, b * ND + dj("y", min(NY - 1, ((g + 1) * GPIX - 1) // YPIX)))
                    bank = act_bank(b, "x1T", g)
                    transposes(bank, [x[:, (GRP * g + k) * TP:(GRP * g + k + 1) * TP] for k in range(GRP)], C, TP).then_inc(act_full, 1)
                experts_to(AT["x1c"])
                channels_back(b, "x1c", x1_normed, x1_normed_act)
                experts_to(AT["score"])
                pe.wait_ge(act_done, b * NA + aj("x1c", NG - 1))
                bank = dve_bank(b, "score")
                for k in range(NT):
                    last = nc.tensor.matmul(bank[0:TP, EXPERTS * k:EXPERTS * (k + 1)], xc[:, k * TP:(k + 1) * TP], gate_w[:, :], start=True, stop=True)
                last.then_inc(dve_full, 1)
                experts_to(AT["gateT"])
                pe.wait_ge(gate_ready, b + 1)
                bank = act_bank(b, "gateT")
                transposes(bank, [gate[:, :, :, :].rearrange("p g e s -> p (g e s)")], TP, NT * EXPERTS).then_inc(act_full, 1)

            def experts(b):
                issued = [0]

                def second(k):
                    g, c = k // NCH, k % NCH
                    e, j = c // CPE, c % CPE
                    pe.wait_ge(hid_act, b * CHUNKS + k + 1)
                    if j == 0:
                        pe.wait_ge(ye_ready, FREE_OUTPUTS + b * OUTPUTS + g * EXPERTS + e - 1)
                    nc.tensor.matmul(py[e % 2][0:C, 0:GPIX], w2[:, c, :], hid[:, k % 3, :], start=(j == 0), stop=(j == CPE - 1)).then_inc(hid_used, 1)

                def issue_to(end):
                    while issued[0] < end:
                        k = issued[0]
                        g, c = k // NCH, k % NCH
                        if c == 0:
                            pe.wait_ge(x_split, b * NG + g + 1)
                        if k >= 2:
                            pe.wait_ge(hid_act, b * CHUNKS + k - 1)
                        cols = slice(c * HCH, (c + 1) * HCH)
                        px = bass.ds(half(b) + g * GPIX, GPIX)
                        bank = ph[k % 2][:, 0:GPIX]
                        nc.tensor.matmul(bank, w1_hi[:, cols], xh[:, px], start=True, stop=False)
                        nc.tensor.matmul(bank, w1_hi[:, cols], xl[:, px], start=False, stop=False)
                        nc.tensor.matmul(bank, w1_lo[:, cols], xh[:, px], start=False, stop=True).then_inc(hid_full, 1)
                        if k >= 1:
                            second(k - 1)
                        issued[0] += 1
                        if issued[0] == CHUNKS:
                            second(k)
                return issue_to

            pe.wait_ge(consts_in, NCONST)
            pe.wait_ge(weights_split, 1)
            attention(0, lambda n: None)
            with pe.Fori(0, BATCH - 1) as b:
                issue_to = experts(b)
                attention(b + 1, issue_to)
                issue_to(CHUNKS)
            experts(BATCH - 1)(CHUNKS)

        @blk.scalar
        def _(act):
            def empty(b, name, g, dst, n, size, scale=1.0):
                j = aj(name, g) - 1
                act.wait_ge(act_full, b * NA + j + 1)
                src = pa[j % 2][0:n, 0:size]
                if len(dst.shape) == 3:
                    src = src.rearrange("p (a c) -> p a c", a=dst.shape[1])
                nc.scalar.activation(dst, src, ACT.Copy, scale=scale).then_inc(act_done, 1)

            def normalise(b, stats, normed):
                act.wait_ge(stats, b + 1)
                for k in range(NORM_DVE * GRP, NT):
                    last = nc.scalar.activation(xT[:, k, :], xT[:, k, :], ACT.Identity, bias=shift[0:TP, k:k + 1], scale=rstd[0:TP, k:k + 1])
                    if k % GRP == GRP - 1:
                        last.then_inc(normed, 1)

            def attention(b, experts_to):
                experts_to(AT["xT"])
                for g in range(NG):
                    empty(b, "xT", g, xT[:, GRP * g:GRP * (g + 1), :], TP, GRP * C)
                experts_to(AT["xc"])
                normalise(b, x_stats, x_normed_act)
                for g in range(NG):
                    r = g * GPIX // W
                    empty(b, "xc", g, xpad[:, 1 + r:1 + r + GPIX // W, 1:1 + W], C, GPIX)
                experts_to(AT["offT"])
                for g in range(2):
                    empty(b, "offT", g, offT[:, 4 * g:4 * g + 4, :], SP, 4 * C)
                experts_to(AT["keyT"])
                for g in range(2):
                    empty(b, "keyT", g, keyT[:, 4 * g:4 * g + 4, :], SP, 4 * C, scale=SCALE)
                experts_to(AT["offc"])
                for g in range(2):
                    j = aj("offc", g) - 1
                    act.wait_ge(act_full, b * NA + j + 1)
                    nc.scalar.activation(offg[:, g * 4 * SP:(g + 1) * 4 * SP], pa[j % 2][0:C, 0:4 * SP], ACT.Gelu, bias=ln_gb[:, 1:2], scale=ln_gb[:, 0:1]).then_inc(act_done, 1)
                experts_to(AT["tanh"])
                act.wait_ge(pos_raw, b + 1)
                nc.scalar.activation(pt[:, :, :], pz[:, :, :], ACT.Tanh).then_inc(pos_tanh, 1)
                experts_to(AT["valT"])
                for g in range(NG):
                    empty(b, "valT", g, valT[:, GRP * g:GRP * (g + 1), :], TP, GRP * C)
                act.wait_ge(act_done, b * NA + aj("valT", NG - 1))
                for start in (0, ODD_BASE * 2 * C - C):
                    act.dma_start(flat[start:start + PIX * C].rearrange("(p k) -> p k", p=TP),
                                  valT[:, :, :].rearrange("p t c -> p (t c)")).then_inc(table_out, 16)
                experts_to(AT["mix"])
                for q in range(QUARTERS):
                    empty(b, "mix", q, mix[:, q, :, :], C, QUARTERS * C)
                experts_to(AT["x1T"])
                for g in range(NG):
                    empty(b, "x1T", g, xT[:, GRP * g:GRP * (g + 1), :], TP, GRP * C)
                experts_to(AT["x1c"])
                normalise(b, x1_stats, x1_normed_act)
                for g in range(NG):
                    empty(b, "x1c", g, xc[:, g * GPIX:(g + 1) * GPIX], C, GPIX)
                experts_to(AT["score"] + 1)
                act.wait_ge(score_ready, b + 1)
                nc.scalar.activation(ex[:, :, :], sc[:, :, :], ACT.Exp).then_inc(score_exp, 1)
                experts_to(AT["gateT"])
                empty(b, "gateT", 0, gateT[:, :], NT * EXPERTS, TP)

            def experts(b):
                done = [0]

                def gelus_to(end):
                    while done[0] < end:
                        k = done[0]
                        act.wait_ge(hid_full, b * CHUNKS + k + 1)
                        nc.scalar.activation(hid[:, k % 3, :], ph[k % 2][:, 0:GPIX], ACT.Gelu, bias=b1[:, k % NCH:k % NCH + 1]).then_inc(hid_act, 1)
                        done[0] += 1
                return gelus_to

            act.wait_ge(pad_zero, 1)
            act.wait_ge(consts_in, NCONST)
            attention(0, lambda n: None)
            with act.Fori(0, BATCH - 1) as b:
                gelus_to = experts(b)
                attention(b + 1, gelus_to)
                gelus_to(CHUNKS)
            experts(BATCH - 1)(CHUNKS)

        @blk.vector
        def _(dve):
            v = nc.vector
            n = [0]

            def step(ins):
                n[0] += 1
                ins.then_inc(dve_step, 1)
                return n[0]

            nc.vector.memset(xpad[:], 0.0).then_inc(pad_zero, 1)
            nc.vector.memset(ye[:, :, 0:1], 0.0).then_inc(ye_ready, FREE_OUTPUTS)
            dve.wait_ge(consts_in, NCONST)
            w1f = w1
            v.tensor_copy(w1_hi[:, :], w1f).then_inc(dve_step, 1)
            dve.wait_ge(dve_step, 1)
            v.tensor_tensor(w1_lo[:, :], w1f, w1_hi[:, :].bitcast(f32), ALU.subtract).then_inc(weights_split, 1)
            BASE = 1

            def attention(b, turn):
                def need(count):
                    dve.wait_ge(dve_step, b * DVE_STEPS + BASE + count)

                def link(ins):
                    need(step(ins))

                def statistics(np_, nt, eps):
                    S = lambda k: st[0:np_, 0:nt, k]
                    A = lambda m: m[0:np_, 0:nt]
                    step(v.tensor_tensor(A(sa), S(1), S(4), ALU.add))
                    step(v.tensor_tensor(A(sd), S(1), S(4), ALU.subtract))
                    link(v.tensor_tensor(A(sv), S(2), S(5), ALU.add))
                    step(v.tensor_scalar(A(mean), A(sa), 0.5, None, ALU.mult))
                    step(v.tensor_tensor(A(sd), A(sd), A(sd), ALU.mult))
                    link(v.tensor_scalar(A(sv), A(sv), 1.0 / C, eps, ALU.mult, ALU.add))
                    link(v.scalar_tensor_tensor(A(sv), A(sd), 0.25, A(sv), ALU.mult, ALU.add))
                    link(v.tensor_scalar(A(si), A(sv).bitcast(i32), 1, None, ALU.logical_shift_right))
                    link(v.tensor_scalar(A(rstd).bitcast(i32), A(si), -1.0, float(0x5F3759DF), ALU.mult, ALU.add))
                    for _ in range(3):
                        link(v.scalar_tensor_tensor(A(su), A(sv), -0.5, A(rstd), ALU.mult, ALU.mult))
                        link(v.tensor_tensor(A(su), A(su), A(rstd), ALU.mult))
                        link(v.scalar_tensor_tensor(A(rstd), A(su), 1.5, A(rstd), ALU.add, ALU.mult))
                    turn(1.9)

                def norm_tokens(name, back, eps, stats, normed):
                    for g in range(NG):
                        dve.wait_ge(act_done, b * NA + aj(name, g))
                        for k in range(GRP * g, GRP * (g + 1)):
                            last = v.bn_stats(st[0:TP, k, :], xT[:, k, :])
                        turn(0.7)
                    link(last)
                    statistics(TP, NT, eps)
                    turn(0.0, back)
                    v.scalar_tensor_tensor(shift[0:TP, :], mean[0:TP, :], -1.0, rstd[0:TP, :], ALU.mult, ALU.mult).then_inc(stats, 1)
                    for k in range(NORM_DVE * GRP):
                        last = v.tensor_scalar(xT[:, k, :], xT[:, k, :], mean[0:TP, k:k + 1], rstd[0:TP, k:k + 1], ALU.subtract, ALU.mult)
                        if k % GRP == GRP - 1:
                            last.then_inc(normed, 1)
                    turn(3.0)

                def conv(i, dst, stride, ready, name, amid=None):
                    for tap in range(TAPS):
                        turn(3.3 if stride == 1 else 0.9, name if tap == TAPS - 1 else None)
                        if tap == 3 and amid:
                            amid()
                        dy, dx = tap // 3, tap % 3
                        src = xpad[:, dy:dy + H:stride, dx:dx + W:stride]
                        if tap == 0:
                            link(v.tensor_scalar(dst, src, conv_w[:, i, 0:1], conv_b[:, i:i + 1], ALU.mult, ALU.add))
                        elif tap < TAPS - 1:
                            link(v.scalar_tensor_tensor(dst, src, conv_w[:, i, tap:tap + 1], dst, ALU.mult, ALU.add))
                        else:
                            v.scalar_tensor_tensor(dst, src, conv_w[:, i, tap:tap + 1], dst, ALU.mult, ALU.add).then_inc(ready, 1)

                def floor(dst, src, big, m=1.0):
                    link(v.tensor_scalar(dst, src, m, 8388608.0, ALU.mult, ALU.add))
                    link(v.tensor_scalar(dst, dst, 8388608.0, None, ALU.subtract))
                    link(v.scalar_tensor_tensor(big, src, m, dst, ALU.mult, ALU.is_lt))
                    link(v.tensor_tensor(dst, dst, big, ALU.subtract))

                n[0] = 0
                norm_tokens("xT", "xc", LN1_EPS, x_stats, x_normed)
                dve.wait_ge(act_done, b * NA + aj("xc", NG - 1))
                conv(0, off, 2, off_conv, "offT")
                conv(1, key[:, :, :], 2, key_conv, "keyT")
                for g in range(2):
                    dve.wait_ge(act_done, b * NA + aj("offT", g))
                    for k in range(4 * g, 4 * g + 4):
                        last = v.bn_stats(st[0:SP, k, :], offT[:, k, :])
                link(last)
                statistics(SP, NS, OFF_EPS)
                turn(3.0, "offc")
                for k in range(NS):
                    last = v.tensor_scalar(offT[:, k, :], offT[:, k, :], mean[0:SP, k:k + 1], rstd[0:SP, k:k + 1], ALU.subtract, ALU.mult)
                last.then_inc(off_normed, 1)
                def raw_positions():
                    dve.wait_ge(dve_full, b * ND + dj("offs"))
                    v.tensor_tensor(pz[:, :, :], pd[0][0:SP, 0:2 * NS].rearrange("p (n k) -> p n k", k=2), ref[:, :, :], ALU.add).then_inc(dve_done, 1)
                    dve.wait_ge(dve_done, b * ND + dj("offs"))
                    turn(0.2, "tanh")
                    v.tensor_copy(gt[:, :, :], pz[:, :, :]).then_inc(pos_raw, 1)

                conv(2, val, 1, val_conv, "valT", amid=raw_positions)
                dve.wait_ge(pos_tanh, b + 1)
                link(v.tensor_scalar(pos[:, :, :], pt[:, :, :], 1.0, 0.5 * (W - 1), ALU.add, ALU.mult))
                floor(fl[:, :, :], pos[:, :, :], gt[:, :, :])
                link(v.tensor_scalar(fl[:, :, :], fl[:, :, :], float(W - 2), None, ALU.min))
                step(v.tensor_tensor(wf[:, :, :], pos[:, :, :], fl[:, :, :], ALU.subtract))
                floor(hx[:, :], fl[:, :, 1], hg[:, :], 0.5)
                link(v.tensor_scalar(ix[:, :], fl[:, :, 1], float(ODD_BASE), None, ALU.mult))
                link(v.scalar_tensor_tensor(ix[:, :], hx[:, :], 1.0 - 2.0 * ODD_BASE, ix[:, :], ALU.mult, ALU.add))
                link(v.scalar_tensor_tensor(ix[:, :], fl[:, :, 0], float(W // 2), ix[:, :], ALU.mult, ALU.add))
                v.tensor_copy(rows[:, 0, :], ix[:, :])
                v.tensor_scalar(rows[:, 1, :], ix[:, :], float(W // 2), None, ALU.add).then_inc(rows_ready, 1)
                link(v.tensor_scalar(wi[:, :, :], wf[:, :, :], -1.0, 1.0, ALU.mult, ALU.add))
                for r, a in enumerate((wi, wf)):
                    for c, d in enumerate((wi, wf)):
                        last = v.tensor_tensor(w4[:, :, r, c], a[:, :, 0], d[:, :, 1], ALU.mult)
                link(last)
                conv(3, query[:, :, :], 1, query_conv, "y")
                turn(0.0, "kv")
                dve.wait_ge(gathered, (b + 1) * 16 * 2 * NS)
                counts = {}
                for r in range(2):
                    for c in range(2):
                        for k in range(NS):
                            w = w4[:, k, r, c:c + 1]
                            if r == c == 0:
                                counts[k] = step(v.tensor_scalar(vs[:, k, :], got[:, k, r, c, :], w, None, ALU.mult))
                                continue
                            need(counts[k])
                            ins = v.scalar_tensor_tensor(vs[:, k, :], got[:, k, r, c, :], w, vs[:, k, :], ALU.mult, ALU.add)
                            if (r, c) != (1, 1):
                                counts[k] = step(ins)
                            elif k % 2:
                                ins.then_inc(sampled, 1)
                turn(6.0)
                for q in range(QUARTERS):
                    dve.wait_ge(dve_full, b * ND + dj("kv", q))
                    v.tensor_tensor(kv[:, q, :, :], pd[(dj("kv", q) - 1) % 2][0:C, 0:QUARTERS * C].rearrange("c (k d) -> c k d", d=C),
                                    head_mask[:, :].rearrange("c (o d) -> c o d", o=1).to_broadcast([C, QUARTERS, C]), ALU.mult).then_inc(dve_done, 1)
                for m in range(NY):
                    dve.wait_ge(dve_full, b * ND + dj("y", m))
                    px = slice(m * YPIX, (m + 1) * YPIX)
                    v.tensor_tensor(x[:, px], pd[(dj("y", m) - 1) % 2][0:C, 0:YPIX], x[:, px], ALU.add).then_inc(dve_done, 1)
                turn(2.0, "x1T")
                norm_tokens("x1T", "x1c", LN2_EPS, x1_stats, x1_normed)
                for g in range(NG):
                    dve.wait_ge(act_done, b * NA + aj("x1c", g))
                    px = slice(g * GPIX, (g + 1) * GPIX)
                    to = bass.ds(half(b) + g * GPIX, GPIX)
                    link(v.tensor_copy(xh[:, to], xc[:, px]))
                    v.tensor_tensor(xl[:, to], xc[:, px], xh[:, to].bitcast(f32), ALU.subtract).then_inc(x_split, 1)
                    turn(0.9)
                turn(2.0)
                turn(0.0, "score")
                dve.wait_ge(dve_full, b * ND + dj("score"))
                full = lambda m: m[:, :].rearrange("p (t o) -> p t o", o=1).to_broadcast([TP, NT, EXPERTS])
                v.tensor_tensor(sc[:, :, :], pd[(dj("score") - 1) % 2][0:TP, 0:NT * EXPERTS].rearrange("p (t e) -> p t e", e=EXPERTS),
                                gate_b[:, :].rearrange("p (o e) -> p o e", o=1).to_broadcast([TP, NT, EXPERTS]), ALU.add).then_inc(dve_done, 1)
                dve.wait_ge(dve_done, b * ND + dj("score"))
                link(v.tensor_reduce(mx[:, :], sc[:, :, :], AX.X, ALU.max))
                v.tensor_tensor(sc[:, :, :], sc[:, :, :], full(mx), ALU.subtract).then_inc(score_ready, 1)
                dve.wait_ge(score_exp, b + 1)
                link(v.tensor_reduce(mx[:, :], ex[:, :, :], AX.X, ALU.add))
                link(v.reciprocal(mx[:, :], mx[:, :]))
                link(v.tensor_tensor(ex[:, :, :], ex[:, :, :], full(mx), ALU.mult))
                for e in range(EXPERTS):
                    last = v.memset(rank[:, :, e], float(e))
                link(last)
                for d in range(1, EXPERTS):
                    m = EXPERTS - d
                    link(v.tensor_tensor(cmp[:, :, 0:m], ex[:, :, d:], ex[:, :, 0:m], ALU.is_gt))
                    link(v.tensor_tensor(rank[:, :, 0:m], rank[:, :, 0:m], cmp[:, :, 0:m], ALU.add))
                    link(v.tensor_tensor(rank[:, :, d:], rank[:, :, d:], cmp[:, :, 0:m], ALU.subtract))
                link(v.scalar_tensor_tensor(ex[:, :, :], rank[:, :, :], 1.5, ex[:, :, :], ALU.is_lt, ALU.mult))
                link(v.tensor_reduce(mx[:, :], ex[:, :, :], AX.X, ALU.add))
                link(v.tensor_scalar(mx[:, :], mx[:, :], 1e-9, None, ALU.add))
                link(v.reciprocal(mx[:, :], mx[:, :]))
                turn(4.0, "gateT")
                v.tensor_tensor(gate[:, :, :, :].rearrange("p g e s -> p g s e"), ex[:, :, :].rearrange("p (g s) e -> p g s e", s=GRP),
                                mx[:, :].rearrange("p (g s o) -> p g s o", s=GRP, o=1).to_broadcast([TP, NG, GRP, EXPERTS]), ALU.mult).then_inc(gate_ready, 1)
                assert n[0] == DVE_STEPS, n[0]

            def experts(b):
                done = [0]

                def outputs_to(end):
                    while done[0] < end:
                        g, e = done[0] // EXPERTS, done[0] % EXPERTS
                        dve.wait_ge(hid_used, b * CHUNKS + (done[0] + 1) * CPE)
                        if e % 2 == 0:
                            dve.wait_ge(gate_in[e // 2], 16 * (b * NG + g + 1))
                        dve.wait_ge(ye_summed, b * OUTPUTS + done[0] + 1)
                        v.scalar_tensor_tensor(ye[:, e, :], py[e % 2][0:C, 0:GPIX], b2[:, e:e + 1], gate_all[:, e, :], ALU.add, ALU.mult).then_inc(ye_ready, 1)
                        done[0] += 1
                return outputs_to

            def beside(outputs_to):
                spent, stage = [0.0], [0]

                def made(name):
                    return max(0, (AT[name] - 1) // CPE)

                def turn(us, name=None):
                    spent[0] += us
                    outputs_to(min(made(WAITED[stage[0]]), max(0, int((spent[0] - OUTPUT_LAG) / OUTPUT_EVERY))))
                    if name:
                        assert WAITED[stage[0]] == name
                        outputs_to(made(name))
                        stage[0] += 1
                return turn

            attention(0, lambda us, name=None: None)
            with dve.Fori(0, BATCH - 1) as b:
                outputs_to = experts(b)
                attention(b + 1, beside(outputs_to))
                outputs_to(OUTPUTS)
            experts(BATCH - 1)(OUTPUTS)

        @blk.gpsimd
        def _(pool):
            p = nc.gpsimd

            def gather(b):
                pool.wait_ge(rows_ready, b + 1)
                pool.wait_ge(table_out, 32 * (b + 1))
                for k in range(NS):
                    for r in range(2):
                        p.indirect_dma_start(got[:, k, r, :, :].rearrange("p a c -> p (a c)"), None, table,
                                             bass.IndirectOffsetOnAxis(ap=rows[:, r, k:k + 1], axis=0)).then_inc(gathered, 16)

            def sum_group(b, g):
                i = b * NG + g
                per = (NG + 1) // 2 if g % 2 == 0 else NG // 2
                wait(pool, res_out[g % 2], 16 * (b * per + g // 2))
                if g == 0:
                    pool.wait_ge(x1_kept, 16 * (b + 1))
                r = res[:, g % 2, :]
                for e in range(EXPERTS):
                    pool.wait_ge(ye_ready, FREE_OUTPUTS + i * EXPERTS + e + 1)
                    ins = p.tensor_tensor(r, x1[:, b % 2, g * GPIX:(g + 1) * GPIX] if e == 0 else r, ye[:, e, :], ALU.add)
                    ins.then_inc(ye_summed, 1)
                    pool.wait_ge(ye_summed, EXPERTS + i * EXPERTS + e + 1)

            p.memset(res[:, :, 0:1], 0.0).then_inc(ye_summed, EXPERTS)
            pool.wait_ge(table_edge, 32)
            gather(0)
            for b in range(BATCH):
                for g in range(NG):
                    sum_group(b, g)
                    if g == 3 and b < BATCH - 1:
                        gather(b + 1)


def kernel(**inputs):
    import numpy as np
    import concourse.bacc as bacc
    from concourse.bass_utils import run_bass_kernel_spmd as run

    f = np.float32
    a = {k: np.asarray(v) for k, v in inputs.items()}
    conv = [("off1"), ("k"), ("v"), ("q")]
    n = np.arange(SAMPLES).reshape(NS, SP).T
    ref = np.stack([(n // WK + 0.5).astype(f) / f(HK) * f(2) - f(1), (n % WK + 0.5).astype(f) / f(WK) * f(2) - f(1)], axis=-1)
    ch = np.arange(C) // CH_PER_HEAD
    arrays = {
        "x": a["x"],
        "ident": np.eye(128, dtype=f),
        "head_mask": (ch[:, None] == ch[None, :]).astype(f),
        "ref": ref.astype(f),
        "conv_w": np.stack([a[f"L0_conv_w_{k}"].reshape(C, TAPS) for k in conv], axis=1),
        "conv_b": np.stack([a[f"L0_conv_b_{k}"] for k in conv], axis=1),
        "ln_gb": np.stack([a["L0_conv_ln_g"], a["L0_conv_ln_b"]], axis=1),
        "woff2": a["L0_conv_w_off2"].T,
        "wout": a["L0_conv_w_out"].T,
        "gate_w": a["L0_ffn_gate_w"],
        "gate_b": a["L0_ffn_gate_b"].reshape(1, EXPERTS),
        "w1": a["L0_ffn_w1"].transpose(1, 0, 2),
        "b1": a["L0_ffn_b1"].reshape(NCH, HCH).T,
        "w2": a["L0_ffn_w2"].reshape(NCH, HCH, C).transpose(1, 0, 2),
        "b2": a["L0_ffn_b2"].T,
    }
    arrays = {"in_" + k: np.ascontiguousarray(v) for k, v in arrays.items()}
    nc = bacc.Bacc("TRN2", target_bir_lowering=False, num_devices=1)
    t = {k[3:]: nc.dram_tensor(k, v.shape, mybir.dt.from_np(v.dtype), kind="ExternalInput").ap() for k, v in arrays.items()}
    out = nc.dram_tensor("out", (BATCH, C, H, W), mybir.dt.float32, kind="ExternalOutput").ap()
    build(nc, t, out)
    r = run(nc, [arrays], core_ids=[0])
    return r.results[0]["out"]
```

```python
import concourse.bass as bass
from concourse import mybir
from contextlib import ExitStack

BATCH, C, H, W = 4, 96, 56, 56
PIX = H * W
HK, WK = H // 2, W // 2
SAMPLES = HK * WK
HEADS, HC = 12, 32
CH_PER_HEAD = C // HEADS
QUARTERS = HC // CH_PER_HEAD
QPIX = PIX // QUARTERS
SCALE = HC ** -0.5
EXPERTS, HID = 4, 4 * C
LN1_EPS, OFF_EPS, LN2_EPS = 1e-6, 1e-5, 1e-5

TP = 112
NT = PIX // TP
GRP = 4
NG = NT // GRP
GPIX = GRP * TP
SP = 98
NS = SAMPLES // SP
YPIX = QPIX // 2
NY = PIX // YPIX
HCH = 128
NCH = EXPERTS * HID // HCH
CPE = HID // HCH
TAPS = 9
OFF, KEY, VALUE, QUERY = range(4)
PAIRS = PIX // 2
ODD_BASE = PAIRS + 1
TABLE_ROWS = ODD_BASE + PAIRS


def jobs(name, number):
    return [(name, g) for g in range(number)]


ACT_HEAD = jobs("xT", NG) + jobs("xc", NG) + jobs("offT", 2) + jobs("keyT", 2) + jobs("offc", 2)
ACT_REST = (jobs("valT", NG) + jobs("xT", NG) + jobs("xc", NG) + jobs("mix", QUARTERS) + jobs("offT", 2)
            + jobs("x1T", NG) + jobs("keyT", 2) + jobs("x1c", NG) + jobs("gateT", 1) + jobs("offc", 2))
DVE_HEAD = jobs("offs", 1)
DVE_REST = jobs("kv", QUARTERS) + jobs("y", NY) + jobs("score", 1) + jobs("offs", 1)
HEAD_STEPS, FIRST_REST_STEPS, REST_STEPS = 71, 134, 154
CHUNKS = NG * NCH
OUTPUTS = NG * EXPERTS
FREE_OUTPUTS = EXPERTS
SPLIT_FIRST = 4
NORM_DVE = 4

GATHER_AFTER = 2

QUERY_AHEAD = 2
VALUE_AHEAD = 2
FIRST_DVE = 4
GATES_US = 4

ROUND = [("valT", 28, 2, 24), ("xT", 39, 2, 0), ("xc", 49, 2, 35), ("kv", 54, 0, 0.5), ("y", 57, 0, 9),
         ("offT", 58, 0, 27), ("x1T", 60, 2, 0.5), ("keyT", 62, 0, 1), ("x1c", 66, 4, 12), ("score", 71, 0, 13),
         ("exp", 74, 0, 4), ("gateT", 79, 0, 9), ("offc", 79, 0, 0), ("offs", 82, 0, 0), ("tanh", 83, 0, 5),
         ("end", 84, 0, 4)]
LAST_ROUND = [("valT", 26, 2, 24), ("kv", 60, 0, 36), ("y", 60, 0, 9), ("x1T", 61, 2, 22), ("x1c", 67, 4, 10),
         ("score", 72, 0, 10), ("exp", 77, 0, 4), ("gateT", 82, 0, 6), ("end", 84, 0, 1)]
OUTPUT_LAG = 1
LAST_ROUND = [("valT", 26, 2, 24), ("kv", 60, 0, 36), ("y", 60, 0, 9), ("x1T", 61, 2, 22),
              ("x1c", 67, 2, 10), ("score", 72, 3, 10), ("exp", 77, 0, 4), ("gateT", 82, 0, 6), ("end", 84, 0, 1)]


class Plan:

    def __init__(self, stages):
        self.start = {name: start for name, start, _, _ in stages}
        self.spread = {name: spread for name, _, spread, _ in stages}
        self.dve_us = {name: us for name, _, _, us in stages if us}
        ends = [0] + [start + spread for _, start, spread, _ in stages]
        assert all(end <= start for end, start in zip(ends, self.start.values())) and ends[-1] <= CHUNKS

    def at(self, name, g=0):
        return self.start[name] + self.spread[name] * g // (NG - 1)

    def needed(self, name):
        return max(0, (self.start[name] + self.spread[name] - 2) // CPE - 1)

    def outputs(self, name):
        made = max(0, (self.start[name] - 1) // CPE)
        number = max(self.needed(name), int((self.start[name] - 1) / CPE - OUTPUT_LAG))
        assert number <= made
        return number


PLAN, LAST_PLAN = Plan(ROUND), Plan(LAST_ROUND)
for plan in (PLAN, LAST_PLAN):
    assert EXPERTS * (GATHER_AFTER + 1) <= plan.outputs("kv")
    assert plan.outputs("valT") < EXPERTS * (GATHER_AFTER + 2)


def build(nc, t, out):
    f32, f32r, i32 = mybir.dt.float32, mybir.dt.float32r, mybir.dt.int32
    ALU, ACT, AX = mybir.AluOpType, mybir.ActivationFunctionType, mybir.AxisListType
    table = nc.dram_tensor("value_table", (TABLE_ROWS, 2 * C), f32, kind="Internal").ap()
    gates = nc.dram_tensor("gate_rows", (BATCH * NG, EXPERTS * GPIX), f32, kind="Internal").ap()
    with ExitStack() as ctx:
        def sb(name, shape, dt=f32):
            return ctx.enter_context(nc.sbuf_tensor(name, shape, dt))

        def pb(name, shape):
            return ctx.enter_context(nc.psum_tensor(name, shape, f32))

        def sem(name):
            return ctx.enter_context(nc.semaphore(name))

        ident = sb("ident", [128, 128])
        head_mask = sb("head_mask", [C, C])
        ref = sb("ref", [SP, NS, 2])
        conv_w = sb("conv_w", [C, 4, TAPS])
        conv_b = sb("conv_b", [C, 4])
        ln_gb = sb("ln_gb", [C, 2])
        woff2 = sb("woff2", [C, 2])
        wout = sb("wout", [C, C])
        gate_w = sb("gate_w", [C, EXPERTS])
        gate_b = sb("gate_b", [TP, EXPERTS])
        w1_hi = sb("w1_hi", [C, EXPERTS * HID], f32r)
        w1_lo = sb("w1_lo", [C, EXPERTS * HID], f32r)
        b1 = sb("b1", [HCH, NCH])
        w2 = sb("w2", [HCH, NCH, C])
        b2 = sb("b2", [C, EXPERTS])
        xs = sb("xs", [C, PIX])
        x = sb("x", [C, PIX])
        xT = sb("xT", [TP, NT, C])
        valT = xT
        xpad = sb("xpad", [C, H + 2, W + 2])
        big = sb("big", [128, PIX])
        w1 = big[0:C, 0:EXPERTS * HID]
        val = big[0:C, :].rearrange("c (h w) -> c h w", h=H)
        got = big[0:SP, 0:NS * 4 * C].rearrange("p (n r a c) -> p n r a c", n=NS, r=2, a=2)
        xc = big[0:C, :]
        query = sb("query", [C, H, W])
        key_area = sb("key_area", [128, SAMPLES])
        key = key_area[0:C, :].rearrange("c (h w) -> c h w", h=HK)
        vs = key_area[0:SP, 0:NS * C].rearrange("p (n c) -> p n c", n=NS)
        keyT = sb("keyT", [SP, NS, C])
        off_area = sb("off_area", [128, 2, 2 * SAMPLES])
        off = off_area[0:C, 0, 0:SAMPLES].rearrange("c (h w) -> c h w", h=HK)
        offT = off_area[0:SP, 0, SAMPLES:SAMPLES + NS * C].rearrange("p (n c) -> p n c", n=NS)
        offg = off_area[0:C, 1, 0:SAMPLES]
        kv = off_area[0:C, 0, 0:QUARTERS * QUARTERS * C].rearrange("c (q k d) -> c q k d", q=QUARTERS, k=QUARTERS)
        mix = off_area[0:C, 1, 0:QUARTERS * QUARTERS * C].rearrange("c (q k d) -> c q k d", q=QUARTERS, k=QUARTERS)
        st = sb("st", [128, NT, 6])
        sa = sb("sa", [128, NT])
        sd = sb("sd", [128, NT])
        sv = sb("sv", [128, NT])
        si = sb("si", [128, NT], i32)
        su = sb("su", [128, NT])
        mean = sb("mean", [128, NT])
        rstd = sb("rstd", [128, NT])
        shift = sb("shift", [128, NT])
        pz = sb("pz", [SP, NS, 2])
        pt = sb("pt", [SP, NS, 2])
        pos = sb("pos", [SP, NS, 2])
        fl = sb("fl", [SP, NS, 2])
        gt = sb("gt", [SP, NS, 2])
        wf = sb("wf", [SP, NS, 2])
        wi = sb("wi", [SP, NS, 2])
        hx = sb("hx", [SP, NS])
        hg = sb("hg", [SP, NS])
        ix = sb("ix", [SP, NS])
        w4 = sb("w4", [SP, NS, 2, 2])
        rows = sb("rows", [SP, 2, NS], i32)
        sc = sb("sc", [TP, NT, EXPERTS])
        ex = sb("ex", [TP, NT, EXPERTS])
        mx = sb("mx", [TP, NT])
        rank = sb("rank", [TP, NT, EXPERTS])
        cmp = sb("cmp", [TP, NT, EXPERTS])
        gate = sb("gate", [TP, NG, EXPERTS, GRP])
        gateT = sb("gateT", [NT * EXPERTS, TP])
        x1 = sb("x1", [C, 2, PIX])
        x_hi = sb("x_hi", [128, 2 * PIX], f32r)
        x_lo = sb("x_lo", [128, 2 * PIX], f32r)
        xh, xl = x_hi[0:C, :], x_lo[0:C, :]
        gate_all = sb("gate_all", [C, EXPERTS, GPIX])
        hid = sb("hid", [HCH, 3, GPIX])
        head_start = sb("head_start", [1, 2])
        ye = sb("ye", [C, EXPERTS, GPIX])
        hid_hi, hid_lo = (m[:, 0:3 * GPIX].rearrange("h (k p) -> h k p", k=3) for m in (x_hi, x_lo))
        w2_hi, w2_lo = (m[:, 3 * GPIX:3 * GPIX + NCH * C].rearrange("h (n c) -> h n c", n=NCH) for m in (x_hi, x_lo))
        assert 3 * GPIX + NCH * C <= (NG - 1) * GPIX
        diag_of = {}
        for i, (m, n) in {KEY: (gate_all, 0), QUERY: (gate_all, 1), VALUE: (ye, 0)}.items():
            flat_m = m[:, :, :].rearrange("c e p -> c (e p)")
            diag_of[i] = flat_m[:, n * TAPS * C:(n + 1) * TAPS * C].rearrange("c (k d) -> c k d", k=TAPS)

        pa = [pb(f"pa{i}", [128, 512]) for i in range(2)]
        pd = [pb(f"pd{i}", [128, 512]) for i in range(2)]
        ph = [pb(f"ph{i}", [128, 512]) for i in range(2)]
        py = [pb(f"py{i}", [128, 512]) for i in range(2)]

        ident_in = sem("ident_in")
        consts_in = sem("consts_in")
        diag_ready = sem("diag_ready")
        conv_full = sem("conv_full")
        conv_done = sem("conv_done")
        weights_split = sem("weights_split")
        xs_in = sem("xs_in")
        x_in = sem("x_in")
        act_full = sem("act_full")
        act_done = sem("act_done")
        dve_full = sem("dve_full")
        dve_done = sem("dve_done")
        dve_step = sem("dve_step")
        x_stats = sem("x_stats")
        x_normed = sem("x_normed")
        x_normed_act = sem("x_normed_act")
        pad_zero = sem("pad_zero")
        off_conv = sem("off_conv")
        key_conv = sem("key_conv")
        val_conv = sem("val_conv")
        query_conv = sem("query_conv")
        off_normed = sem("off_normed")
        pos_raw = sem("pos_raw")
        pos_tanh = sem("pos_tanh")
        rows_ready = sem("rows_ready")
        table_out = sem("table_out")
        table_edge = sem("table_edge")
        gathered = sem("gathered")
        sampled = sem("sampled")
        x1_stats = sem("x1_stats")
        x1_normed = sem("x1_normed")
        x1_normed_act = sem("x1_normed_act")
        x1_kept = sem("x1_kept")
        score_ready = sem("score_ready")
        score_exp = sem("score_exp")
        gate_ready = sem("gate_ready")
        gate_out = sem("gate_out")
        gate_in = [sem(f"gate_in{i}") for i in range(2)]
        x_split = sem("x_split")
        hid_full = sem("hid_full")
        hid_act = sem("hid_act")
        hid_used = sem("hid_used")
        ye_ready = sem("ye_ready")
        ye_summed = sem("ye_summed")
        w2_part = sem("w2_part")
        w2_split = sem("w2_split")
        hid_hi_ready = sem("hid_hi_ready")
        hid_lo_ready = sem("hid_lo_ready")
        res_out = [sem(f"res_out{i}") for i in range(2)]

        consts = [(head_mask, "head_mask"), (ref, "ref"), (conv_w, "conv_w"),
                  (conv_b, "conv_b"), (ln_gb, "ln_gb"), (woff2, "woff2"), (wout, "wout"),
                  (gate_w, "gate_w"), (b1, "b1"), (b2, "b2"), (w1.rearrange("c (e h) -> c e h", e=EXPERTS), "w1"), (w2, "w2")]
        NCONST = 16 * (len(consts) + 1)

        def job(head, rest, b, name, g=0):
            last = [j for j in rest if j not in head]
            static = isinstance(b, int)
            if (name, g) not in head:
                order = last if static and b == BATCH - 1 else rest
                i = order.index((name, g)) + len(head)
            elif static and b == 0:
                i = head.index((name, g))
            else:
                i, b = rest.index((name, g)) + len(head), b - 1
            return i % 2, b * len(rest) + i + 1

        assert len(ACT_REST) % 2 == len(DVE_REST) % 2 == 0

        def first(b):
            return isinstance(b, int) and b == 0

        def act_job(b, name, g=0):
            return job(ACT_HEAD, ACT_REST, b, name, g)

        def dve_job(b, name, g=0):
            return job(DVE_HEAD, DVE_REST, b, name, g)

        def acted(b, name, g=0):
            return act_job(b, name, g)[1]

        def dved(b, name, g=0):
            return dve_job(b, name, g)[1]

        first_convs = ([(KEY, 2, g) for g in range(2)] + [(VALUE, 1, g) for g in range(FIRST_DVE, NG)]
                       + [(QUERY, 1, g) for g in range(FIRST_DVE, NG)])
        last_value = 2 + NG - FIRST_DVE

        def group_rows(stride):
            return HK // 2 if stride == 2 else H // NG

        flat = table.rearrange("r c -> (r c)")
        x_rows = t["x"].rearrange("b c h w -> (b c) (h w)")
        out_rows = out.rearrange("b c h w -> (b c) (h w)")

        def gate_rows(b):
            return gates[bass.ds(b * NG, NG), :].rearrange("g (r p) -> (g r) p", p=TP)

        def wait(eng, semaphore, value):
            if not (isinstance(value, int) and value <= 0):
                eng.wait_ge(semaphore, value)

        def half(b):
            return (b % 2) * PIX

        blk = ctx.enter_context(nc.Block())

        @blk.sync
        def _(sp):
            def load_xs(b):
                if b < BATCH:
                    if b > 0:
                        sp.wait_ge(act_done, acted(b - 1, "xT", NG - 1))
                    sp.dma_start(xs[:, :], x_rows[b * C:(b + 1) * C, :]).then_inc(xs_in, 16)

            def load_x(b):
                if b < BATCH:
                    if b > 0:
                        sp.wait_ge(x1_kept, 16 * b)
                        sp.wait_ge(act_done, acted(b - 1, "x1T", NG - 1))
                    sp.dma_start(x[:, :], x_rows[b * C:(b + 1) * C, :]).then_inc(x_in, 16)

            def keep_x1(b):
                sp.wait_ge(dve_done, dved(b, "y", NY - 1))
                wait(sp, res_out[b % 2], 16 * NG * (b // 2))
                sp.dma_start(x1[:, b % 2, :], x[:, :]).then_inc(x1_kept, 16)

            def load_gates(b, g):
                if g == 0:
                    sp.wait_ge(gate_out, 16 * (b + 1))
                for k in range(2):
                    sp.wait_ge(ye_ready, FREE_OUTPUTS + b * OUTPUTS + EXPERTS * (g - 1) + 2 * k + 2)
                    sp.dma_start(gate_all[:, 2 * k:2 * k + 2, :].rearrange("c e p -> c (e p)"),
                                 gates[b * NG + g:b * NG + g + 1, 2 * k * GPIX:(2 * k + 2) * GPIX].to_broadcast([C, 2 * GPIX])).then_inc(gate_in[k], 16)

            def store_result(b, g):
                sp.wait_ge(ye_summed, EXPERTS + b * OUTPUTS + EXPERTS * (g + 1))
                sp.dma_start(out_rows[b * C:(b + 1) * C, g * GPIX:(g + 1) * GPIX], x1[:, b % 2, g * GPIX:(g + 1) * GPIX]).then_inc(res_out[b % 2], 16)

            sp.dma_start(ident[:, :], t["ident"]).then_inc(ident_in, 16)
            load_xs(0)
            for dst, name in consts:
                sp.dma_start(dst if name == "w1" else dst[:], t[name]).then_inc(consts_in, 16)
            sp.dma_start(gate_b[:, :], t["gate_b"].to_broadcast([TP, EXPERTS])).then_inc(consts_in, 16)
            sp.wait_ge(pad_zero, 1)
            for start in (PIX * C, TABLE_ROWS * 2 * C - C):
                sp.dma_start(flat[start:start + C].rearrange("(c o) -> c o", o=1), xpad[:, 0, 0:1]).then_inc(table_edge, 16)
            load_x(0)
            load_xs(1)
            load_xs(2)
            keep_x1(0)
            load_x(1)
            load_gates(0, 0)
            for b in range(BATCH):
                for g in range(NG):
                    if g < NG - 1:
                        load_gates(b, g + 1)
                    elif b < BATCH - 1:
                        load_xs(b + 3)
                        keep_x1(b + 1)
                        load_x(b + 2)
                        load_gates(b + 1, 0)
                    store_result(b, g)
            for parity in range(2):
                sp.wait_ge(res_out[parity], 16 * NG * (BATCH // 2))

        @blk.tensor
        def _(pe):
            def act_bank(b, name, g=0):
                i, done = act_job(b, name, g)
                wait(pe, act_done, done - 2)
                return pa[i]

            def dve_bank(b, name, g=0):
                i, done = dve_job(b, name, g)
                wait(pe, dve_done, done - 2)
                return pd[i]

            def transposes(bank, ins, size, n):
                for k, piece in enumerate(ins):
                    last = nc.tensor.transpose(bank[0:n, k * size:(k + 1) * size], piece, ident[0:size, 0:size])
                return last

            def channels_back(b, name, normed, normed_act, before=lambda g: None):
                for g in range(NG):
                    before(g)
                    if g < NORM_DVE:
                        pe.wait_ge(normed, b * NORM_DVE + g + 1)
                    else:
                        pe.wait_ge(normed_act, b * (NG - NORM_DVE) + g - NORM_DVE + 1)
                    bank = act_bank(b, name, g)
                    transposes(bank, [xT[:, GRP * g + k, :] for k in range(GRP)], TP, C).then_inc(act_full, 1)

            def x_to_tokens(b, before=lambda g: None):
                pe.wait_ge(xs_in, b * 16 + 16)
                for g in range(NG):
                    before(g)
                    bank = act_bank(b, "xT", g)
                    transposes(bank, [xs[:, (GRP * g + k) * TP:(GRP * g + k + 1) * TP] for k in range(GRP)], C, TP).then_inc(act_full, 1)

            def to_samples(b, name, src, ready, count):
                pe.wait_ge(ready, count)
                src = src.rearrange("c h w -> c (h w)")
                for g in range(2):
                    bank = act_bank(b, name, g)
                    transposes(bank, [src[:, (4 * g + k) * SP:(4 * g + k + 1) * SP] for k in range(4)], C, SP).then_inc(act_full, 1)

            def convolve(number):
                for n in range(convolved[0], convolved[0] + number):
                    i, stride, g = first_convs[n]
                    if n >= 2:
                        pe.wait_ge(conv_done, n - 1)
                    m = group_rows(stride)
                    bank = ph[n % 2][0:C, 0:m * (W // stride)].rearrange("c (h w) -> c h w", h=m)
                    for k in range(TAPS):
                        dy, dx = k // 3 + g * m * stride, k % 3
                        last = nc.tensor.matmul(bank, diag_of[i][:, k, :], xpad[:, dy:dy + m * stride:stride, dx:dx + W:stride],
                                                start=(k == 0), stop=(k == TAPS - 1))
                    last.then_inc(conv_full, 1)
                convolved[0] += number

            convolved = [0]

            def off_to_channels(b):
                pe.wait_ge(off_normed, b + 1)
                for g in range(2):
                    bank = act_bank(b, "offc", g)
                    transposes(bank, [offT[:, 4 * g + k, :] for k in range(4)], SP, C).then_inc(act_full, 1)

            def offsets(b):
                if first(b):
                    pe.wait_ge(consts_in, NCONST)
                pe.wait_ge(act_done, acted(b, "offc", 1))
                bank = dve_bank(b, "offs")
                for k in range(NS):
                    last = nc.tensor.matmul(bank[0:SP, 2 * k:2 * k + 2], offg[:, k * SP:(k + 1) * SP], woff2[:, :], start=True, stop=True)
                last.then_inc(dve_full, 1)

            def head(b):
                x_to_tokens(b)
                channels_back(b, "xc", x_normed, x_normed_act)
                pe.wait_ge(act_done, acted(b, "xc", NG - 1))
                pe.wait_ge(diag_ready, 3)
                convolve(2)
                to_samples(b, "offT", off, off_conv, 1)
                to_samples(b, "keyT", key, conv_done, 2)
                convolve(1)
                off_to_channels(b)
                convolve(1)
                offsets(b)
                convolve(1)

            def rest(b, with_head, plan, chunks_to):
                chunks_to(plan.at("valT"))
                pe.wait_ge(val_conv, b + 1)
                if first(b):
                    pe.wait_ge(conv_done, last_value)
                valf = val.rearrange("c h w -> c (h w)").rearrange("c (p t) -> c t p", t=NT)
                for g in range(NG):
                    chunks_to(plan.at("valT", g))
                    bank = act_bank(b, "valT", g)
                    transposes(bank, [valf[:, GRP * g + k, :] for k in range(GRP)], C, TP).then_inc(act_full, 1)
                if first(b):
                    convolve(2)
                if with_head:
                    chunks_to(plan.at("xT"))
                    x_to_tokens(b + 1, lambda g: chunks_to(plan.at("xT", g)))
                    if first(b):
                        convolve(1)
                    chunks_to(plan.at("xc"))
                    channels_back(b + 1, "xc", x_normed, x_normed_act, lambda g: chunks_to(plan.at("xc", g)))
                chunks_to(plan.at("kv"))
                keyq = keyT[:, :, :].rearrange("p (q h) c -> p h q c", h=2)
                for q in range(QUARTERS):
                    pe.wait_ge(sampled, b * QUARTERS + q + 1)
                    bank = dve_bank(b, "kv", q)
                    for h in range(2):
                        last = nc.tensor.matmul(bank[0:C, 0:QUARTERS * C], vs[:, 2 * q + h, :], keyq[:, h], start=(h == 0), stop=(h == 1))
                    last.then_inc(dve_full, 1)
                for q in range(QUARTERS):
                    pe.wait_ge(dve_done, dved(b, "kv", q))
                    bank = act_bank(b, "mix", q)
                    for k in range(QUARTERS):
                        last = nc.tensor.matmul(bank[0:C, k * C:(k + 1) * C], kv[:, q, k, :], wout[:, :], start=True, stop=True)
                    last.then_inc(act_full, 1)
                chunks_to(plan.at("y"))
                if first(b):
                    pe.wait_ge(conv_done, len(first_convs))
                pe.wait_ge(query_conv, b + 1)
                queryf = query[:, :, :].rearrange("c h w -> c (h w)")
                for n in range(NY):
                    q, h = n // 2, n % 2
                    pe.wait_ge(act_done, acted(b, "mix", q))
                    bank = dve_bank(b, "y", n)
                    for k in range(QUARTERS):
                        last = nc.tensor.matmul(bank[0:C, 0:YPIX], mix[:, q, k, :], queryf[:, k * QPIX + h * YPIX:k * QPIX + (h + 1) * YPIX],
                                                start=(k == 0), stop=(k == QUARTERS - 1))
                    last.then_inc(dve_full, 1)
                if with_head:
                    chunks_to(plan.at("offT"))
                    to_samples(b + 1, "offT", off, off_conv, b + 2)
                chunks_to(plan.at("x1T"))
                for g in range(NG):
                    chunks_to(plan.at("x1T", g))
                    pe.wait_ge(dve_done, dved(b, "y", min(NY - 1, ((g + 1) * GPIX - 1) // YPIX)))
                    bank = act_bank(b, "x1T", g)
                    transposes(bank, [x[:, (GRP * g + k) * TP:(GRP * g + k + 1) * TP] for k in range(GRP)], C, TP).then_inc(act_full, 1)
                if with_head:
                    chunks_to(plan.at("keyT"))
                    to_samples(b + 1, "keyT", key, key_conv, b + 1)
                chunks_to(plan.at("x1c"))
                score_bank = dve_bank(b, "score")

                def scores(g):
                    pe.wait_ge(act_done, acted(b, "x1c", g))
                    for k in range(GRP * g, GRP * (g + 1)):
                        last = nc.tensor.matmul(score_bank[0:TP, EXPERTS * k:EXPERTS * (k + 1)], xc[:, k * TP:(k + 1) * TP], gate_w[:, :], start=True, stop=True)
                    return last

                def before_x1c(g):
                    if g >= 3:
                        scores(g - 3)
                    chunks_to(plan.at("x1c", g))

                channels_back(b, "x1c", x1_normed, x1_normed_act, before_x1c)
                for g in range(NG - 3, NG):
                    if g == NG - 1:
                        chunks_to(plan.at("score"))
                    last = scores(g)
                last.then_inc(dve_full, 1)
                chunks_to(plan.at("gateT"))
                pe.wait_ge(gate_ready, b + 1)
                bank = act_bank(b, "gateT")
                transposes(bank, [gate[:, :, :, :].rearrange("p g e s -> p (g e s)")], TP, NT * EXPERTS).then_inc(act_full, 1)
                if with_head:
                    chunks_to(plan.at("offc"))
                    off_to_channels(b + 1)
                    chunks_to(plan.at("offs"))
                    offsets(b + 1)

            def experts(b):
                issued = [0]

                def second(k):
                    g, c = k // NCH, k % NCH
                    e, j = c // CPE, c % CPE
                    pe.wait_ge(hid_act, b * CHUNKS + k + 1)
                    if j == 0:
                        pe.wait_ge(ye_ready, FREE_OUTPUTS + b * OUTPUTS + g * EXPERTS + e - 1)
                    nc.tensor.matmul(py[e % 2][0:C, 0:GPIX], w2[:, c, :], hid[:, k % 3, :], start=(j == 0), stop=(j == CPE - 1)).then_inc(hid_used, 1)

                def issue_to(end):
                    while issued[0] < end:
                        k = issued[0]
                        g, c = k // NCH, k % NCH
                        if c == 0:
                            pe.wait_ge(x_split, b * NG + g + 1)
                        if k >= 2:
                            pe.wait_ge(hid_act, b * CHUNKS + k - 1)
                        cols = slice(c * HCH, (c + 1) * HCH)
                        px = bass.ds(half(b) + g * GPIX, GPIX)
                        bank = ph[k % 2][:, 0:GPIX]
                        nc.tensor.matmul(bank, w1_hi[:, cols], xh[:, px], start=True, stop=False)
                        nc.tensor.matmul(bank, w1_hi[:, cols], xl[:, px], start=False, stop=False)
                        nc.tensor.matmul(bank, w1_lo[:, cols], xh[:, px], start=False, stop=True).then_inc(hid_full, 1)
                        if k >= 1:
                            second(k - 1)
                        issued[0] += 1
                        if issued[0] == CHUNKS:
                            second(k)
                return issue_to

            def last_experts(b):
                def first_product(k):
                    g, c = k // NCH, k % NCH
                    if c == 0:
                        pe.wait_ge(x_split, b * NG + g + 1)
                    if k >= 2:
                        pe.wait_ge(hid_act, b * CHUNKS + k - 1)
                    cols = slice(c * HCH, (c + 1) * HCH)
                    px = slice(half(b) + g * GPIX, half(b) + (g + 1) * GPIX)
                    bank = ph[k % 2][:, 0:GPIX]
                    nc.tensor.matmul(bank, w1_hi[:, cols], xh[:, px], start=True, stop=False)
                    nc.tensor.matmul(bank, w1_hi[:, cols], xl[:, px], start=False, stop=False)
                    nc.tensor.matmul(bank, w1_lo[:, cols], xh[:, px], start=False, stop=True).then_inc(hid_full, 1)

                def second_product(k):
                    g, c = k // NCH, k % NCH
                    e, j = c // CPE, c % CPE
                    if j == 0:
                        pe.wait_ge(ye_ready, FREE_OUTPUTS + b * OUTPUTS + g * EXPERTS + e - 1)
                    bank = py[e % 2][0:C, 0:GPIX]
                    pe.wait_ge(hid_hi_ready, k + 1)
                    nc.tensor.matmul(bank, w2_hi[:, c, :], hid_hi[:, k % 3, :], start=(j == 0), stop=False)
                    nc.tensor.matmul(bank, w2_lo[:, c, :], hid_hi[:, k % 3, :], start=False, stop=False)
                    pe.wait_ge(hid_lo_ready, k + 1)
                    nc.tensor.matmul(bank, w2_hi[:, c, :], hid_lo[:, k % 3, :], start=False, stop=(j == CPE - 1)).then_inc(hid_used, 1)

                pe.wait_ge(w2_split, 1)
                first_product(0)
                first_product(1)
                for k in range(2, CHUNKS):
                    first_product(k)
                    second_product(k - 2)
                second_product(CHUNKS - 2)
                second_product(CHUNKS - 1)

            pe.wait_ge(ident_in, 16)
            head(0)
            pe.wait_ge(consts_in, NCONST)
            pe.wait_ge(weights_split, 1)
            rest(0, True, PLAN, lambda number: None)
            with pe.Fori(0, BATCH - 2) as b:
                issue_to = experts(b)
                rest(b + 1, True, PLAN, issue_to)
                issue_to(CHUNKS)
            issue_to = experts(BATCH - 2)
            rest(BATCH - 1, False, LAST_PLAN, issue_to)
            issue_to(CHUNKS)
            last_experts(BATCH - 1)

        @blk.scalar
        def _(act):
            def empty(b, name, g, dst, n, size, scale=1.0):
                i, full = act_job(b, name, g)
                act.wait_ge(act_full, full)
                src = pa[i][0:n, 0:size]
                if len(dst.shape) == 3:
                    src = src.rearrange("p (a c) -> p a c", a=dst.shape[1])
                nc.scalar.activation(dst, src, ACT.Copy, scale=scale).then_inc(act_done, 1)

            def normalise(b, stats, normed, job):
                act.wait_ge(stats, b + 1)
                for g in range(NG):
                    if NORM_DVE + g < NG:
                        for k in range((NORM_DVE + g) * GRP, (NORM_DVE + g + 1) * GRP):
                            last = nc.scalar.activation(xT[:, k, :], xT[:, k, :], ACT.Identity, bias=shift[0:TP, k:k + 1], scale=rstd[0:TP, k:k + 1])
                        last.then_inc(normed, 1)
                    job(g)

            def x_to_tokens(b, before=lambda g: None):
                for g in range(NG):
                    before(g)
                    empty(b, "xT", g, xT[:, GRP * g:GRP * (g + 1), :], TP, GRP * C)

            def padded(b, before=lambda g: None):
                def job(g):
                    before(g)
                    r = g * GPIX // W
                    empty(b, "xc", g, xpad[:, 1 + r:1 + r + GPIX // W, 1:1 + W], C, GPIX)
                normalise(b, x_stats, x_normed_act, job)

            def off_to_samples(b):
                for g in range(2):
                    empty(b, "offT", g, offT[:, 4 * g:4 * g + 4, :], SP, 4 * C)

            def key_to_samples(b):
                for g in range(2):
                    empty(b, "keyT", g, keyT[:, 4 * g:4 * g + 4, :], SP, 4 * C, scale=SCALE)

            def off_gelu(b):
                for g in range(2):
                    i, full = act_job(b, "offc", g)
                    act.wait_ge(act_full, full)
                    nc.scalar.activation(offg[:, g * 4 * SP:(g + 1) * 4 * SP], pa[i][0:C, 0:4 * SP], ACT.Gelu, bias=ln_gb[:, 1:2], scale=ln_gb[:, 0:1]).then_inc(act_done, 1)

            def limit_positions(b):
                act.wait_ge(pos_raw, b + 1)
                nc.scalar.activation(pt[:, :, :], pz[:, :, :], ACT.Tanh).then_inc(pos_tanh, 1)

            def convolved(start, end):
                for n in range(start, end):
                    i, stride, g = first_convs[n]
                    m = group_rows(stride)
                    dst = {KEY: key, VALUE: val, QUERY: query[:, :, :]}[i][:, g * m:(g + 1) * m, :]
                    act.wait_ge(conv_full, n + 1)
                    nc.scalar.activation(dst, ph[n % 2][0:C, 0:m * (W // stride)].rearrange("c (h w) -> c h w", h=m),
                                         ACT.Identity, bias=conv_b[:, i:i + 1]).then_inc(conv_done, 1)

            def head(b):
                x_to_tokens(b)
                act.wait_ge(pad_zero, 1)
                padded(b)
                act.wait_ge(consts_in, NCONST)
                convolved(0, 2)
                off_to_samples(b)
                key_to_samples(b)
                convolved(2, 3)
                off_gelu(b)
                convolved(3, 4)
                limit_positions(b)
                convolved(4, 5)

            def rest(b, with_head, plan, gelus_to):
                gelus_to(plan.at("valT"))
                for g in range(NG):
                    gelus_to(plan.at("valT", g))
                    empty(b, "valT", g, valT[:, GRP * g:GRP * (g + 1), :], TP, GRP * C)
                act.wait_ge(act_done, acted(b, "valT", NG - 1))
                for start in (0, ODD_BASE * 2 * C - C):
                    act.dma_start(flat[start:start + PIX * C].rearrange("(p k) -> p k", p=TP),
                                  valT[:, :, :].rearrange("p t c -> p (t c)")).then_inc(table_out, 16)
                if first(b):
                    convolved(5, 7)
                if with_head:
                    gelus_to(plan.at("xT"))
                    act.wait_ge(table_out, 32 * (b + 1))
                    x_to_tokens(b + 1, lambda g: gelus_to(plan.at("xT", g)))
                    if first(b):
                        convolved(7, 8)
                    gelus_to(plan.at("xc"))
                    padded(b + 1, lambda g: gelus_to(plan.at("xc", g)))
                gelus_to(plan.at("kv"))
                for q in range(QUARTERS):
                    empty(b, "mix", q, mix[:, q, :, :], C, QUARTERS * C)
                if with_head:
                    gelus_to(plan.at("offT"))
                    off_to_samples(b + 1)
                gelus_to(plan.at("x1T"))
                for g in range(NG):
                    gelus_to(plan.at("x1T", g))
                    empty(b, "x1T", g, xT[:, GRP * g:GRP * (g + 1), :], TP, GRP * C)
                if with_head:
                    gelus_to(plan.at("keyT"))
                    key_to_samples(b + 1)
                gelus_to(plan.at("x1c"))
                def channels(g):
                    gelus_to(plan.at("x1c", g))
                    empty(b, "x1c", g, xc[:, g * GPIX:(g + 1) * GPIX], C, GPIX)
                normalise(b, x1_stats, x1_normed_act, channels)
                gelus_to(plan.at("exp"))
                act.wait_ge(score_ready, b + 1)
                nc.scalar.activation(ex[:, :, :], sc[:, :, :], ACT.Exp).then_inc(score_exp, 1)
                gelus_to(plan.at("gateT"))
                empty(b, "gateT", 0, gateT[:, :], NT * EXPERTS, TP)
                act.wait_ge(act_done, acted(b, "gateT"))
                act.dma_start(gate_rows(b), gateT[:, :]).then_inc(gate_out, 16)
                if with_head:
                    gelus_to(plan.at("offc"))
                    off_gelu(b + 1)
                    gelus_to(plan.at("tanh"))
                    limit_positions(b + 1)

            def experts(b):
                done = [0]

                def gelus_to(end):
                    while done[0] < end:
                        k = done[0]
                        act.wait_ge(hid_full, b * CHUNKS + k + 1)
                        nc.scalar.activation(hid[:, k % 3, :], ph[k % 2][:, 0:GPIX], ACT.Gelu, bias=b1[:, k % NCH:k % NCH + 1]).then_inc(hid_act, 1)
                        done[0] += 1
                return gelus_to

            def last_experts(b):
                for k in range(CHUNKS):
                    act.wait_ge(hid_full, b * CHUNKS + k + 1)
                    for dst, ready in ((hid_hi, hid_hi_ready), (hid, hid_act)):
                        nc.scalar.activation(dst[:, k % 3, :], ph[k % 2][:, 0:GPIX], ACT.Gelu, bias=b1[:, k % NCH:k % NCH + 1]).then_inc(ready, 1)

            head(0)
            rest(0, True, PLAN, lambda number: None)
            with act.Fori(0, BATCH - 2) as b:
                gelus_to = experts(b)
                rest(b + 1, True, PLAN, gelus_to)
                gelus_to(CHUNKS)
            gelus_to = experts(BATCH - 2)
            rest(BATCH - 1, False, LAST_PLAN, gelus_to)
            gelus_to(CHUNKS)
            last_experts(BATCH - 1)

        @blk.vector
        def _(dve):
            v = nc.vector
            n = [0]

            def step(ins):
                n[0] += 1
                ins.then_inc(dve_step, 1)
                return n[0]

            nc.vector.memset(xpad[:], 0.0).then_inc(pad_zero, 1)
            nc.vector.memset(head_start[:, 0:1], 0.0).then_inc(ye_ready, FREE_OUTPUTS)

            base = [0]

            def need(count):
                dve.wait_ge(dve_step, base[0] + count)

            def link(ins):
                need(step(ins))

            def statistics(np_, nt, eps, turn):
                S = lambda k: st[0:np_, 0:nt, k]
                A = lambda m: m[0:np_, 0:nt]
                step(v.tensor_tensor(A(sa), S(1), S(4), ALU.add))
                step(v.tensor_tensor(A(sd), S(1), S(4), ALU.subtract))
                link(v.tensor_tensor(A(sv), S(2), S(5), ALU.add))
                step(v.tensor_scalar(A(mean), A(sa), 0.5, None, ALU.mult))
                step(v.tensor_tensor(A(sd), A(sd), A(sd), ALU.mult))
                link(v.tensor_scalar(A(sv), A(sv), 1.0 / C, eps, ALU.mult, ALU.add))
                link(v.scalar_tensor_tensor(A(sv), A(sd), 0.25, A(sv), ALU.mult, ALU.add))
                link(v.tensor_scalar(A(si), A(sv).bitcast(i32), 1, None, ALU.logical_shift_right))
                link(v.tensor_scalar(A(rstd).bitcast(i32), A(si), -1.0, float(0x5F3759DF), ALU.mult, ALU.add))
                for _ in range(3):
                    link(v.scalar_tensor_tensor(A(su), A(sv), -0.5, A(rstd), ALU.mult, ALU.mult))
                    link(v.tensor_tensor(A(su), A(su), A(rstd), ALU.mult))
                    link(v.scalar_tensor_tensor(A(rstd), A(su), 1.5, A(rstd), ALU.add, ALU.mult))
                turn(1.9)

            def norm_tokens(b, name, back, eps, stats, normed, turn):
                for g in range(NG):
                    dve.wait_ge(act_done, acted(b, name, g))
                    for k in range(GRP * g, GRP * (g + 1)):
                        last = v.bn_stats(st[0:TP, k, :], xT[:, k, :])
                    turn(0.7)
                link(last)
                statistics(TP, NT, eps, turn)
                turn(0.0, back)
                v.scalar_tensor_tensor(shift[0:TP, :], mean[0:TP, :], -1.0, rstd[0:TP, :], ALU.mult, ALU.mult).then_inc(stats, 1)
                for k in range(NORM_DVE * GRP):
                    last = v.tensor_scalar(xT[:, k, :], xT[:, k, :], mean[0:TP, k:k + 1], rstd[0:TP, k:k + 1], ALU.subtract, ALU.mult)
                    if k % GRP == GRP - 1:
                        last.then_inc(normed, 1)
                turn(3.0)

            def tap(i, k, dst, stride, ready, rows_=H):
                dy, dx = k // 3, k % 3
                src = xpad[:, dy:dy + rows_:stride, dx:dx + W:stride]
                if k == 0:
                    link(v.tensor_scalar(dst, src, conv_w[:, i, 0:1], conv_b[:, i:i + 1], ALU.mult, ALU.add))
                elif k < TAPS - 1:
                    link(v.scalar_tensor_tensor(dst, src, conv_w[:, i, k:k + 1], dst, ALU.mult, ALU.add))
                else:
                    v.scalar_tensor_tensor(dst, src, conv_w[:, i, k:k + 1], dst, ALU.mult, ALU.add).then_inc(ready, 1)

            def off_key_tap(k):
                if k < TAPS:
                    tap(OFF, k, off, 2, off_conv)
                else:
                    tap(KEY, k - TAPS, key, 2, key_conv)

            def floor(dst, src, big, m=1.0):
                link(v.tensor_scalar(dst, src, m, 8388608.0, ALU.mult, ALU.add))
                link(v.tensor_scalar(dst, dst, 8388608.0, None, ALU.subtract))
                link(v.scalar_tensor_tensor(big, src, m, dst, ALU.mult, ALU.is_lt))
                link(v.tensor_tensor(dst, dst, big, ALU.subtract))

            def normalise_off(b, turn):
                for g in range(2):
                    dve.wait_ge(act_done, acted(b, "offT", g))
                    for k in range(4 * g, 4 * g + 4):
                        last = v.bn_stats(st[0:SP, k, :], offT[:, k, :])
                link(last)
                statistics(SP, NS, OFF_EPS, turn)
                turn(3.0)
                for k in range(NS):
                    last = v.tensor_scalar(offT[:, k, :], offT[:, k, :], mean[0:SP, k:k + 1], rstd[0:SP, k:k + 1], ALU.subtract, ALU.mult)
                last.then_inc(off_normed, 1)

            def raw_positions(b, turn):
                turn(0.0, "offc")
                turn(0.0, "offs")
                dve.wait_ge(dve_full, dved(b, "offs"))
                v.tensor_tensor(pz[:, :, :], pd[dve_job(b, "offs")[0]][0:SP, 0:2 * NS].rearrange("p (n k) -> p n k", k=2), ref[:, :, :], ALU.add).then_inc(dve_done, 1)
                dve.wait_ge(dve_done, dved(b, "offs"))
                turn(0.2, "tanh")
                v.tensor_copy(gt[:, :, :], pz[:, :, :]).then_inc(pos_raw, 1)

            def positions(b):
                dve.wait_ge(pos_tanh, b + 1)
                link(v.tensor_scalar(pos[:, :, :], pt[:, :, :], 1.0, 0.5 * (W - 1), ALU.add, ALU.mult))
                floor(fl[:, :, :], pos[:, :, :], gt[:, :, :])
                link(v.tensor_scalar(fl[:, :, :], fl[:, :, :], float(W - 2), None, ALU.min))
                step(v.tensor_tensor(wf[:, :, :], pos[:, :, :], fl[:, :, :], ALU.subtract))
                floor(hx[:, :], fl[:, :, 1], hg[:, :], 0.5)
                link(v.tensor_scalar(ix[:, :], fl[:, :, 1], float(ODD_BASE), None, ALU.mult))
                link(v.scalar_tensor_tensor(ix[:, :], hx[:, :], 1.0 - 2.0 * ODD_BASE, ix[:, :], ALU.mult, ALU.add))
                link(v.scalar_tensor_tensor(ix[:, :], fl[:, :, 0], float(W // 2), ix[:, :], ALU.mult, ALU.add))
                v.tensor_copy(rows[:, 0, :], ix[:, :])
                v.tensor_scalar(rows[:, 1, :], ix[:, :], float(W // 2), None, ALU.add).then_inc(rows_ready, 1)
                link(v.tensor_scalar(wi[:, :, :], wf[:, :, :], -1.0, 1.0, ALU.mult, ALU.add))
                for r, a in enumerate((wi, wf)):
                    for c, d in enumerate((wi, wf)):
                        last = v.tensor_tensor(w4[:, :, r, c], a[:, :, 0], d[:, :, 1], ALU.mult)
                link(last)

            def dve_rows(b):
                return FIRST_DVE * GPIX // W if first(b) else H

            def value_tap(b, k):
                m = dve_rows(b)
                tap(VALUE, k, val[:, 0:m, :], 1, val_conv, m)

            def query_tap(b, k):
                m = dve_rows(b)
                tap(QUERY, k, query[:, 0:m, :], 1, query_conv, m)

            def head(b):
                norm_tokens(b, "xT", "xc", LN1_EPS, x_stats, x_normed, no_turn)
                dve.wait_ge(consts_in, NCONST)
                link(v.tensor_copy(w1_hi[:, :], w1))
                v.tensor_tensor(w1_lo[:, :], w1, w1_hi[:, :].bitcast(f32), ALU.subtract).then_inc(weights_split, 1)
                dve.wait_ge(act_done, acted(b, "xc", NG - 1))
                for k in range(TAPS):
                    off_key_tap(k)
                value_tap(b, 0)
                normalise_off(b, no_turn)
                for k in range(1, 6):
                    value_tap(b, k)
                raw_positions(b, no_turn)
                for k in range(6, TAPS):
                    value_tap(b, k)
                positions(b)
                assert n[0] == HEAD_STEPS, n[0]

            def rest(b, with_head, turn):
                n[0] = 0
                base[0] = HEAD_STEPS if first(b) else b * REST_STEPS + HEAD_STEPS + FIRST_REST_STEPS - REST_STEPS
                for k in range(TAPS if first(b) else VALUE_AHEAD, TAPS):
                    turn(3.3, "valT" if k == TAPS - 1 else None)
                    value_tap(b, k)
                    if k == VALUE_AHEAD:
                        positions(b)
                for k in range(0 if first(b) else QUERY_AHEAD, TAPS):
                    turn(3.3)
                    query_tap(b, k)
                if with_head:
                    turn(0.0, "xT")
                    norm_tokens(b + 1, "xT", "xc", LN1_EPS, x_stats, x_normed, turn)
                turn(6.0, "kv")
                dve.wait_ge(gathered, (b + 1) * 16 * 2 * NS)
                counts = {}
                for r in range(2):
                    for c in range(2):
                        for k in range(NS):
                            w = w4[:, k, r, c:c + 1]
                            if r == c == 0:
                                counts[k] = step(v.tensor_scalar(vs[:, k, :], got[:, k, r, c, :], w, None, ALU.mult))
                                continue
                            need(counts[k])
                            ins = v.scalar_tensor_tensor(vs[:, k, :], got[:, k, r, c, :], w, vs[:, k, :], ALU.mult, ALU.add)
                            if (r, c) != (1, 1):
                                counts[k] = step(ins)
                            elif k % 2:
                                ins.then_inc(sampled, 1)
                for q in range(QUARTERS):
                    dve.wait_ge(dve_full, dved(b, "kv", q))
                    v.tensor_tensor(kv[:, q, :, :], pd[dve_job(b, "kv", q)[0]][0:C, 0:QUARTERS * C].rearrange("c (k d) -> c k d", d=C),
                                    head_mask[:, :].rearrange("c (o d) -> c o d", o=1).to_broadcast([C, QUARTERS, C]), ALU.mult).then_inc(dve_done, 1)
                turn(0.0, "y")
                dve.wait_ge(x_in, (b + 1) * 16)
                if with_head:
                    dve.wait_ge(act_done, acted(b + 1, "xc", NG - 1))
                    dve.wait_ge(act_full, acted(b, "mix", QUARTERS - 1))
                for m in range(NY):
                    if with_head:
                        off_key_tap(2 * m)
                        off_key_tap(2 * m + 1)
                    dve.wait_ge(dve_full, dved(b, "y", m))
                    px = slice(m * YPIX, (m + 1) * YPIX)
                    v.tensor_tensor(x[:, px], pd[dve_job(b, "y", m)[0]][0:C, 0:YPIX], x[:, px], ALU.add).then_inc(dve_done, 1)
                if with_head:
                    off_key_tap(2 * NY)
                    off_key_tap(2 * NY + 1)
                    turn(0.0, "offT")
                turn(0.0, "x1T")
                if with_head:
                    turn(0.0, "keyT")
                norm_tokens(b, "x1T", "x1c", LN2_EPS, x1_stats, x1_normed, turn)
                if with_head:
                    dve.wait_ge(x1_normed_act, (b + 1) * (NG - NORM_DVE))
                    normalise_off(b + 1, turn)

                def split_x(groups):
                    for g in groups:
                        dve.wait_ge(act_done, acted(b, "x1c", g))
                        px = slice(g * GPIX, (g + 1) * GPIX)
                        to = bass.ds(half(b) + g * GPIX, GPIX)
                        link(v.tensor_copy(xh[:, to], xc[:, px]))
                        v.tensor_tensor(xl[:, to], xc[:, px], xh[:, to].bitcast(f32), ALU.subtract).then_inc(x_split, 1)
                        turn(0.9)

                split_x(range(SPLIT_FIRST))
                turn(0.0, "score")
                dve.wait_ge(dve_full, dved(b, "score"))
                full = lambda m: m[:, :].rearrange("p (t o) -> p t o", o=1).to_broadcast([TP, NT, EXPERTS])
                v.tensor_tensor(sc[:, :, :], pd[dve_job(b, "score")[0]][0:TP, 0:NT * EXPERTS].rearrange("p (t e) -> p t e", e=EXPERTS),
                                gate_b[:, :].rearrange("p (o e) -> p o e", o=1).to_broadcast([TP, NT, EXPERTS]), ALU.add).then_inc(dve_done, 1)
                dve.wait_ge(dve_done, dved(b, "score"))
                link(v.tensor_reduce(mx[:, :], sc[:, :, :], AX.X, ALU.max))
                turn(0.8, "exp")
                v.tensor_tensor(sc[:, :, :], sc[:, :, :], full(mx), ALU.subtract).then_inc(score_ready, 1)
                split_x(range(SPLIT_FIRST, NG))
                for e in range(EXPERTS):
                    last = v.memset(rank[:, :, e], float(e))
                link(last)
                dve.wait_ge(score_exp, b + 1)
                link(v.tensor_reduce(mx[:, :], ex[:, :, :], AX.X, ALU.add))
                link(v.reciprocal(mx[:, :], mx[:, :]))
                link(v.tensor_tensor(ex[:, :, :], ex[:, :, :], full(mx), ALU.mult))
                for d in range(1, EXPERTS):
                    m = EXPERTS - d
                    link(v.tensor_tensor(cmp[:, :, 0:m], ex[:, :, d:], ex[:, :, 0:m], ALU.is_gt))
                    link(v.tensor_tensor(rank[:, :, 0:m], rank[:, :, 0:m], cmp[:, :, 0:m], ALU.add))
                    link(v.tensor_tensor(rank[:, :, d:], rank[:, :, d:], cmp[:, :, 0:m], ALU.subtract))
                link(v.scalar_tensor_tensor(ex[:, :, :], rank[:, :, :], 1.5, ex[:, :, :], ALU.is_lt, ALU.mult))
                link(v.tensor_reduce(mx[:, :], ex[:, :, :], AX.X, ALU.add))
                link(v.tensor_scalar(mx[:, :], mx[:, :], 1e-9, None, ALU.add))
                link(v.reciprocal(mx[:, :], mx[:, :]))
                turn(2.5, "gateT")
                v.tensor_tensor(gate[:, :, :, :].rearrange("p g e s -> p g s e"), ex[:, :, :].rearrange("p (g s) e -> p g s e", s=GRP),
                                mx[:, :].rearrange("p (g s o) -> p g s o", s=GRP, o=1).to_broadcast([TP, NG, GRP, EXPERTS]), ALU.mult).then_inc(gate_ready, 1)
                if with_head:
                    for k in range(QUERY_AHEAD):
                        turn(3.3)
                        query_tap(b + 1, k)
                    for k in range(VALUE_AHEAD):
                        turn(3.3)
                        value_tap(b + 1, k)
                        if k == 0:
                            raw_positions(b + 1, turn)
                turn(0.0, "end")
                assert not with_head or n[0] == (FIRST_REST_STEPS if first(b) else REST_STEPS), n[0]

            def experts(b):
                done = [0]

                def outputs_to(end):
                    while done[0] < end:
                        g, e = done[0] // EXPERTS, done[0] % EXPERTS
                        dve.wait_ge(hid_used, b * CHUNKS + (done[0] + 1) * CPE)
                        if e % 2 == 0:
                            dve.wait_ge(gate_in[e // 2], 16 * (b * NG + g + 1))
                        dve.wait_ge(ye_summed, b * OUTPUTS + done[0] + 1)
                        v.scalar_tensor_tensor(ye[:, e, :], py[e % 2][0:C, 0:GPIX], b2[:, e:e + 1], gate_all[:, e, :], ALU.add, ALU.mult).then_inc(ye_ready, 1)
                        done[0] += 1
                return outputs_to

            def beside(plan, outputs_to):
                stages = list(plan.dve_us)
                at, spent = [0], [0.0]

                def turn(us, name=None):
                    spent[0] += us
                    if at[0] < len(stages):
                        this = stages[at[0]]
                        before = plan.outputs(stages[at[0] - 1]) if at[0] else 0
                        late = 0 if at[0] else GATES_US
                        part = min(1.0, max(0.0, spent[0] - late) / max(plan.dve_us[this] - late, 1.0))
                        outputs_to(round(before + (plan.outputs(this) - before) * part))
                    if name and name not in plan.dve_us:
                        outputs_to(plan.needed(name))
                    elif name:
                        assert this == name, (this, name)
                        outputs_to(plan.outputs(name))
                        at[0] += 1
                        spent[0] = 0.0
                return turn

            def split_w2():
                dve.wait_ge(hid_full, (BATCH - 1) * CHUNKS - NCH + 1)
                v.tensor_copy(w2_hi, w2[:, :, :]).then_inc(w2_part, 1)
                dve.wait_ge(w2_part, 1)
                v.tensor_tensor(w2_lo, w2[:, :, :], w2_hi.bitcast(f32), ALU.subtract).then_inc(w2_split, 1)

            def last_experts(b):
                outputs_to = experts(b)
                for k in range(CHUNKS):
                    dve.wait_ge(hid_act, b * CHUNKS + k + 1)
                    v.tensor_tensor(hid_lo[:, k % 3, :], hid[:, k % 3, :], hid_hi[:, k % 3, :].bitcast(f32), ALU.subtract).then_inc(hid_lo_ready, 1)
                    if k >= CPE + 1 and (k - 1) % CPE == 0:
                        outputs_to((k - 1) // CPE)
                outputs_to(OUTPUTS)

            def no_turn(us, name=None):
                pass

            head(0)
            rest(0, True, no_turn)
            with dve.Fori(0, BATCH - 2) as b:
                outputs_to = experts(b)
                rest(b + 1, True, beside(PLAN, outputs_to))
                outputs_to(OUTPUTS)
            outputs_to = experts(BATCH - 2)
            rest(BATCH - 1, False, beside(LAST_PLAN, outputs_to))
            outputs_to(OUTPUTS - EXPERTS)
            split_w2()
            outputs_to(OUTPUTS)
            last_experts(BATCH - 1)

        @blk.gpsimd
        def _(pool):
            p = nc.gpsimd

            def gather(b):
                pool.wait_ge(rows_ready, b + 1)
                pool.wait_ge(table_out, 32 * (b + 1))
                for k in range(NS):
                    for r in range(2):
                        p.indirect_dma_start(got[:, k, r, :, :].rearrange("p a c -> p (a c)"), None, table,
                                             bass.IndirectOffsetOnAxis(ap=rows[:, r, k:k + 1], axis=0)).then_inc(gathered, 16)

            def sum_group(b, g):
                i = b * NG + g
                if g == 0:
                    pool.wait_ge(x1_kept, 16 * (b + 1))
                r = x1[:, b % 2, g * GPIX:(g + 1) * GPIX]
                for e in range(EXPERTS):
                    pool.wait_ge(ye_ready, FREE_OUTPUTS + i * EXPERTS + e + 1)
                    ins = p.tensor_tensor(r, r, ye[:, e, :], ALU.add)
                    ins.then_inc(ye_summed, 1)
                    pool.wait_ge(ye_summed, EXPERTS + i * EXPERTS + e + 1)

            p.memset(head_start[:, 1:2], 0.0).then_inc(ye_summed, EXPERTS)
            pool.wait_ge(ident_in, 16)
            pool.wait_ge(consts_in, NCONST)
            for i in (KEY, VALUE, QUERY):
                p.tensor_tensor(diag_of[i], ident[0:C, 0:C].rearrange("c (o d) -> c o d", o=1).to_broadcast([C, TAPS, C]),
                                conv_w[:, i, :].rearrange("c (k o) -> c k o", o=1).to_broadcast([C, TAPS, C]), ALU.mult).then_inc(diag_ready, 1)
            pool.wait_ge(table_edge, 32)
            gather(0)
            for b in range(BATCH):
                for g in range(NG):
                    sum_group(b, g)
                    if g == GATHER_AFTER and b < BATCH - 1:
                        gather(b + 1)


def kernel(**inputs):
    import numpy as np
    import concourse.bacc as bacc
    from concourse.bass_utils import run_bass_kernel_spmd as run

    f = np.float32
    a = {k: np.asarray(v) for k, v in inputs.items()}
    conv = [("off1"), ("k"), ("v"), ("q")]
    n = np.arange(SAMPLES).reshape(NS, SP).T
    ref = np.stack([(n // WK + 0.5).astype(f) / f(HK) * f(2) - f(1), (n % WK + 0.5).astype(f) / f(WK) * f(2) - f(1)], axis=-1)
    ch = np.arange(C) // CH_PER_HEAD
    arrays = {
        "x": a["x"],
        "ident": np.eye(128, dtype=f),
        "head_mask": (ch[:, None] == ch[None, :]).astype(f),
        "ref": ref.astype(f),
        "conv_w": np.stack([a[f"L0_conv_w_{k}"].reshape(C, TAPS) for k in conv], axis=1),
        "conv_b": np.stack([a[f"L0_conv_b_{k}"] for k in conv], axis=1),
        "ln_gb": np.stack([a["L0_conv_ln_g"], a["L0_conv_ln_b"]], axis=1),
        "woff2": a["L0_conv_w_off2"].T,
        "wout": a["L0_conv_w_out"].T,
        "gate_w": a["L0_ffn_gate_w"],
        "gate_b": a["L0_ffn_gate_b"].reshape(1, EXPERTS),
        "w1": a["L0_ffn_w1"].transpose(1, 0, 2),
        "b1": a["L0_ffn_b1"].reshape(NCH, HCH).T,
        "w2": a["L0_ffn_w2"].reshape(NCH, HCH, C).transpose(1, 0, 2),
        "b2": a["L0_ffn_b2"].T,
    }
    arrays = {"in_" + k: np.ascontiguousarray(v) for k, v in arrays.items()}
    nc = bacc.Bacc("TRN2", target_bir_lowering=False, num_devices=1)
    t = {k[3:]: nc.dram_tensor(k, v.shape, mybir.dt.from_np(v.dtype), kind="ExternalInput").ap() for k, v in arrays.items()}
    out = nc.dram_tensor("out", (BATCH, C, H, W), mybir.dt.float32, kind="ExternalOutput").ap()
    build(nc, t, out)
    r = run(nc, [arrays], core_ids=[0])
    return r.results[0]["out"]
```
